# Optimizing a Trainium2 kernel written in Bass

```python
import numpy as np
import jax
import jax.numpy as jnp

def _softmax(x, axis=-1):
    return jax.nn.softmax(x, axis=axis)

def _gelu(x):
    return jax.nn.gelu(x, approximate=True)

def _silu(x):
    return jax.nn.silu(x)

def _sigmoid(x):
    return jax.nn.sigmoid(x)

def _layernorm(x, axis=-1, eps=1e-05):
    m = jnp.mean(x, axis=axis, keepdims=True)
    v = jnp.var(x, axis=axis, keepdims=True)
    return (x - m) / jnp.sqrt(v + eps)

def _scatter_add(tgt, idx, src, axis=0):
    return tgt.at[idx].add(src)

def _segment_sum(src, seg, n):
    return jax.ops.segment_sum(src, seg, n)
kernel_name = 'mk_audio_tower_d2_tok_audfeat1024_r4_2c8c79'

def setup_inputs(seed: int=0):
    np.random.seed(seed)
    _w = jnp.asarray

    def _rec_inputs():
        import jax
        import jax.numpy as jnp
        _rk = jax.random.key(seed)
        x = 0.00021031 + 1.00007 * jax.random.normal(jax.random.fold_in(_rk, 1), (16, 256, 256), jnp.float32)
        return x
    x = _rec_inputs()

    def _L0_tok_setup():
        import jax, jax.numpy as jnp
        import numpy as np
        DIM = 256
        SEGMENT_SIZE = 256
        DILATION_RATE = 2
        key = jax.random.key(seed)
        x = jax.random.normal(key, (4, 2048, DIM), dtype=jnp.float32)
        return {'x': x}
    _L0_tok_all = _L0_tok_setup()
    _L0_tok_in = {k: v for k, v in _L0_tok_all.items() if k in ()}
    del _L0_tok_all

    def _L0_attn_setup():
        import math
        import jax, jax.numpy as jnp
        import numpy as np
        B, S, E, H = (4, 512, 256, 16)
        HD = E // H
        key = jax.random.key(seed)
        ks = jax.random.split(key, 7)
        scale = 1.0 / math.sqrt(E)
        return {'x': jax.random.normal(ks[0], (B, S, E), dtype=jnp.float32), 'Wq': jax.random.normal(ks[1], (H, HD, E), dtype=jnp.float32) * scale, 'bq': jax.random.normal(ks[2], (H, HD), dtype=jnp.float32) * 0.01, 'Wk': jax.random.normal(ks[3], (H, HD, E), dtype=jnp.float32) * scale, 'bk': jax.random.normal(ks[4], (H, HD), dtype=jnp.float32) * 0.01, 'Wv': jax.random.normal(ks[5], (H, HD, E), dtype=jnp.float32) * scale, 'bv': jax.random.normal(ks[6], (H, HD), dtype=jnp.float32) * 0.01}
    _L0_attn_all = _L0_attn_setup()
    _L0_attn_in = {k: v for k, v in _L0_attn_all.items() if k in ('Wq', 'bq', 'Wk', 'bk', 'Wv', 'bv')}
    del _L0_attn_all

    def _L0_ffn_setup():
        import jax, jax.numpy as jnp
        import numpy as np
        D = 256
        I = 128
        E = 32
        K = 4
        T = 2 * 512
        C = 2 * T * K // E
        key = jax.random.key(seed)
        ks = jax.random.split(key, 9)
        bf = jnp.bfloat16
        std = 0.02
        x = jax.random.normal(ks[0], (2, 512, D), dtype=jnp.float32).astype(bf)
        gate_w = (std * jax.random.normal(ks[1], (E, D), dtype=jnp.float32)).astype(bf)
        bias = jnp.zeros((E,), jnp.float32)
        W1 = (std * jax.random.normal(ks[2], (E, D, I), dtype=jnp.float32)).astype(bf)
        W3 = (std * jax.random.normal(ks[3], (E, D, I), dtype=jnp.float32)).astype(bf)
        W2 = (std * jax.random.normal(ks[4], (E, I, D), dtype=jnp.float32)).astype(bf)
        sw1 = (std * jax.random.normal(ks[5], (I, D), dtype=jnp.float32)).astype(bf)
        sw3 = (std * jax.random.normal(ks[6], (I, D), dtype=jnp.float32)).astype(bf)
        sw2 = (std * jax.random.normal(ks[7], (D, I), dtype=jnp.float32)).astype(bf)
        return {'x': x, 'gate_w': gate_w, 'bias': bias, 'W1': W1, 'W3': W3, 'W2': W2, 'sw1': sw1, 'sw3': sw3, 'sw2': sw2}
    _L0_ffn_all = _L0_ffn_setup()
    _L0_ffn_in = {k: v for k, v in _L0_ffn_all.items() if k in ('gate_w', 'bias', 'W1', 'W3', 'W2', 'sw1', 'sw3', 'sw2')}
    del _L0_ffn_all

    def _L1_attn_setup():
        import jax, jax.numpy as jnp
        import numpy as np
        B, S, D = (4, 512, 256)
        key = jax.random.key(seed)
        k1, k2, k3, k4 = jax.random.split(key, 4)
        x = jax.random.normal(k1, (B, S, D), dtype=jnp.float32)
        Qw = jax.random.normal(k2, (D, D), dtype=jnp.float32) / 40
        Kw = jax.random.normal(k3, (D, D), dtype=jnp.float32) / 40
        Vw = jax.random.normal(k4, (D, D), dtype=jnp.float32) / 40
        return {'x': x, 'Qw': Qw, 'Kw': Kw, 'Vw': Vw}
    _L1_attn_all = _L1_attn_setup()
    _L1_attn_in = {k: v for k, v in _L1_attn_all.items() if k in ('Qw', 'Kw', 'Vw')}
    del _L1_attn_all

    def _L1_ffn_setup():
        import jax, jax.numpy as jnp
        import numpy as np
        NUM_EXPERTS = 8
        TOP_K = 2
        CAP_RATIO = 1.25
        INIT_STD = 0.02
        key = jax.random.key(seed)
        k1, k2, k3, k4 = jax.random.split(key, 4)
        B, T, H, F = (4, 512, 256, 1024)
        x = jax.random.normal(k1, (B, T, H), jnp.float32)
        router_w = jax.random.normal(k2, (NUM_EXPERTS, H), jnp.float32) * INIT_STD
        w1 = jax.random.normal(k3, (NUM_EXPERTS, H, F), jnp.float32) * INIT_STD
        w2 = jax.random.normal(k4, (NUM_EXPERTS, F, H), jnp.float32) * INIT_STD
        return {'x': x, 'router_w': router_w, 'w1': w1, 'w2': w2}
    _L1_ffn_all = _L1_ffn_setup()
    _L1_ffn_in = {k: v for k, v in _L1_ffn_all.items() if k in ('router_w', 'w1', 'w2')}
    del _L1_ffn_all
    return {'x': x, 'L0_attn_Wq': _L0_attn_in['Wq'], 'L0_attn_bq': _L0_attn_in['bq'], 'L0_attn_Wk': _L0_attn_in['Wk'], 'L0_attn_bk': _L0_attn_in['bk'], 'L0_attn_Wv': _L0_attn_in['Wv'], 'L0_attn_bv': _L0_attn_in['bv'], 'L0_ffn_gate_w': _L0_ffn_in['gate_w'], 'L0_ffn_bias': _L0_ffn_in['bias'], 'L0_ffn_W1': _L0_ffn_in['W1'], 'L0_ffn_W3': _L0_ffn_in['W3'], 'L0_ffn_W2': _L0_ffn_in['W2'], 'L0_ffn_sw1': _L0_ffn_in['sw1'], 'L0_ffn_sw3': _L0_ffn_in['sw3'], 'L0_ffn_sw2': _L0_ffn_in['sw2'], 'L1_attn_Qw': _L1_attn_in['Qw'], 'L1_attn_Kw': _L1_attn_in['Kw'], 'L1_attn_Vw': _L1_attn_in['Vw'], 'L1_ffn_router_w': _L1_ffn_in['router_w'], 'L1_ffn_w1': _L1_ffn_in['w1'], 'L1_ffn_w2': _L1_ffn_in['w2']}

def reference(x, L0_attn_Wq, L0_attn_bq, L0_attn_Wk, L0_attn_bk, L0_attn_Wv, L0_attn_bv, L0_ffn_gate_w, L0_ffn_bias, L0_ffn_W1, L0_ffn_W3, L0_ffn_W2, L0_ffn_sw1, L0_ffn_sw3, L0_ffn_sw2, L1_attn_Qw, L1_attn_Kw, L1_attn_Vw, L1_ffn_router_w, L1_ffn_w1, L1_ffn_w2):
    import jax
    import jax.numpy as jnp

    def _L0_tok_ref(x):
        import jax, jax.numpy as jnp
        import numpy as np
        DIM = 256
        SEGMENT_SIZE = 256
        DILATION_RATE = 2
        B, S, D = x.shape
        pad = -S % SEGMENT_SIZE
        x = jnp.pad(x, ((0, 0), (0, pad), (0, 0)))
        x = x.reshape(B, -1, SEGMENT_SIZE, D)
        x = x[:, :, ::DILATION_RATE, :]
        q = k = v = x
        scale = 1.0 / jnp.sqrt(jnp.asarray(D, dtype=x.dtype))
        scores = jnp.einsum('bsqd,bskd->bsqk', q, k) * scale
        probs = jax.nn.softmax(scores, axis=-1)
        attn = jnp.einsum('bsqk,bskd->bsqd', probs, v)
        return attn.reshape(B, -1, D)

    def _L0_attn_ref(x, Wq, bq, Wk, bk, Wv, bv):
        import math
        import jax, jax.numpy as jnp
        import numpy as np
        B, S, E, H = (4, 512, 256, 16)
        HD = E // H
        b, s, e = x.shape
        h, hd, _ = Wq.shape
        inv_scale = 1.0 / math.sqrt(hd)
        q = jnp.einsum('bse,hde->bshd', x, Wq) + bq
        k = jnp.einsum('bse,hde->bshd', x, Wk) + bk
        v = jnp.einsum('bse,hde->bshd', x, Wv) + bv
        mask = jnp.triu(jnp.full((s, s), -jnp.inf, dtype=x.dtype), k=1)
        scores = (jnp.einsum('bqhd,bkhd->bhqk', q, k) + mask) * inv_scale
        attn = jax.nn.softmax(scores, axis=-1)
        out = jnp.einsum('bhqk,bkhd->bqhd', attn, v)
        return out.reshape(b, s, h * hd)

    def _L0_ffn_ref(x, gate_w, bias, W1, W3, W2, sw1, sw3, sw2):
        import jax, jax.numpy as jnp
        import numpy as np
        D = 256
        I = 128
        E = 32
        K = 4
        T = 2 * 512
        C = 2 * T * K // E
        X = x.reshape(-1, D)
        logits = (X @ gate_w.T).astype(jnp.float32)
        scores = jax.nn.sigmoid(logits)
        _, idx = jax.lax.top_k(scores + bias[None, :], K)
        w = jnp.take_along_axis(scores, idx, axis=-1)
        w = w / jnp.clip(jnp.sum(w, axis=-1, keepdims=True), 1e-12, None)
        w = w.astype(x.dtype)
        eid = idx.reshape(-1)
        onehot = (eid[:, None] == jnp.arange(E)[None, :]).astype(jnp.int32)
        pos = jnp.take_along_axis(jnp.cumsum(onehot, axis=0) - 1, eid[:, None], axis=1)[:, 0]
        valid = pos < C
        posc = jnp.minimum(pos, C - 1)
        Xrep = jnp.repeat(X, K, axis=0)
        xe = jnp.zeros((E, C, D), x.dtype).at[eid, posc].add(jnp.where(valid[:, None], Xrep, jnp.zeros((), x.dtype)))
        h = jax.nn.silu(jnp.einsum('ecd,edi->eci', xe, W1)) * jnp.einsum('ecd,edi->eci', xe, W3)
        ye = jnp.einsum('eci,eid->ecd', h, W2)
        gflat = jnp.where(valid, w.reshape(-1), jnp.zeros((), x.dtype))
        yrows = ye[eid, posc] * gflat[:, None]
        out = yrows.reshape(-1, K, D).sum(axis=1)
        out = out + jax.nn.silu(X @ sw1.T) * (X @ sw3.T) @ sw2.T
        return out.reshape(x.shape)

    def _L1_attn_ref(x, Qw, Kw, Vw):
        import jax, jax.numpy as jnp
        import numpy as np
        B, S, D = (4, 512, 256)
        Q = x @ Qw
        K = x @ Kw
        V = x @ Vw
        d = x.shape[-1]
        S_len = x.shape[-2]
        mask = jnp.where(jnp.tril(jnp.ones((S_len, S_len), dtype=x.dtype)) == 0, -jnp.inf, 0.0).astype(x.dtype)
        scores = jnp.einsum('bqd,bkd->bqk', Q, K) / jnp.sqrt(jnp.asarray(d, x.dtype))
        scores = scores + mask
        attn = jax.nn.softmax(scores, axis=-1)
        return jnp.einsum('bqk,bkd->bqd', attn, V)

    def _L1_ffn_ref(x, router_w, w1, w2):
        import jax, jax.numpy as jnp
        import numpy as np
        NUM_EXPERTS = 8
        TOP_K = 2
        CAP_RATIO = 1.25
        INIT_STD = 0.02
        B, T, H = x.shape
        E, K = (NUM_EXPERTS, TOP_K)
        xf = x.reshape(-1, H)
        N = xf.shape[0]
        P = N * K
        capacity = int(CAP_RATio * N * K / E) + 1 if False else int(CAP_RATIO * N * K / E) + 1
        logits = xf @ router_w.T
        probs = jax.nn.softmax(logits, axis=-1)
        k_probs, k_idx = jax.lax.top_k(probs, K)
        k_probs = k_probs / jnp.sum(k_probs, axis=-1, keepdims=True)
        flat_e = k_idx.reshape(-1)
        onehot = jax.nn.one_hot(flat_e, E, dtype=jnp.int32)
        rank = jnp.take_along_axis(jnp.cumsum(onehot, axis=0) - 1, flat_e[:, None], axis=1)[:, 0]
        keep = rank < capacity
        slot = jnp.minimum(rank, capacity - 1)
        token_id = jnp.arange(P) // K
        dispatched = jnp.where(keep[:, None], xf[token_id], 0.0)
        buf = jnp.zeros((E, capacity, H), x.dtype).at[flat_e, slot].add(dispatched)
        h = jax.nn.silu(jnp.einsum('ech,ehf->ecf', buf, w1))
        out_buf = jnp.einsum('ecf,efh->ech', h, w2)
        pair_out = out_buf[flat_e, slot] * keep[:, None].astype(x.dtype)
        combined = jnp.sum(pair_out.reshape(N, K, H) * k_probs[..., None], axis=1)
        return combined.reshape(B, T, H) + x
    h = _L0_tok_ref(x)
    h = h + _L0_attn_ref(_layernorm(h, axis=-1), L0_attn_Wq, L0_attn_bq, L0_attn_Wk, L0_attn_bk, L0_attn_Wv, L0_attn_bv)
    h = h + _L0_ffn_ref(_layernorm(h, axis=-1), L0_ffn_gate_w, L0_ffn_bias, L0_ffn_W1, L0_ffn_W3, L0_ffn_W2, L0_ffn_sw1, L0_ffn_sw3, L0_ffn_sw2)
    h = h + _L1_attn_ref(_layernorm(h, axis=-1), L1_attn_Qw, L1_attn_Kw, L1_attn_Vw)
    h = h + _L1_ffn_ref(_layernorm(h, axis=-1), L1_ffn_router_w, L1_ffn_w1, L1_ffn_w2)
    return h

_drawn_inputs = setup_inputs


def setup_inputs(seed=0):
    import zlib

    import numpy as np

    out = dict(_drawn_inputs(seed))
    spreads = {'L0_ffn_bias': (0.0, 0.8)}
    factors = {'L0_attn_bq': 8.0,
     'L0_attn_bk': 64.0,
     'L0_attn_bv': 5.158,
     'L0_ffn_gate_w': 8.0,
     'L0_ffn_W1': 8.0,
     'L0_ffn_W3': 8.0,
     'L0_ffn_W2': 8.0,
     'L0_ffn_sw1': 4.811,
     'L0_ffn_sw3': 4.733,
     'L0_ffn_sw2': 4.772,
     'L1_attn_Qw': 5.295,
     'L1_attn_Kw': 5.196,
     'L1_ffn_router_w': 3.676,
     'L1_ffn_w1': 3.254,
     'L1_ffn_w2': 3.217}
    for name, (base, spread) in spreads.items():
        noise = np.random.default_rng([zlib.crc32(name.encode()), seed]).standard_normal(out[name].shape)
        drawn = base * np.exp(spread * noise) if base else spread * noise
        out[name] = jnp.asarray(drawn.astype(out[name].dtype))
    for name, factor in factors.items():
        out[name] = (out[name] * factor).astype(out[name].dtype)
    return out
```

```python
from contextlib import ExitStack

import concourse.bass as bass
from concourse import mybir

ALU = mybir.AluOpType
ACT = mybir.ActivationFunctionType
AX = mybir.AxisListType
F32 = mybir.dt.float32
F32R = mybir.dt.float32r
BF16 = mybir.dt.bfloat16
U32 = mybir.dt.uint32
I32 = mybir.dt.int32

P = 128
TILES = 16
D = 256
KD = D // P
TOKENS = TILES * P
HEADS, HEAD = 16, 16
GROUPS = 4
E0, K0, CAP0, I0 = 32, 4, 256, 128
E1, K1, CAP1, I1 = 8, 2, 641, 1024
STRIDE1 = 768
SLOTS1 = 656
FC1 = I1 // P
EPS = 1e-5
MASKED = -3e38
PAD0, PAD = 256, 1024


class Sems:

    def __init__(self, nc):
        self.nc, self.made, self.half = nc, {}, ""

    def __call__(self, name):
        if name not in self.made:
            self.made[name] = self.nc.alloc_semaphore(name + self.half)
        return self.made[name]

    def clear(self):
        self.nc.clear_and_free_semaphores(list(self.made.values()))
        self.nc.all_engine_barrier()
        self.made, self.half = {}, "_2"


class Tile:

    def __init__(self, loop, const):
        self.loop, self.const = loop, const
        self.t = const if loop is None else loop * 2 + const
        self.par = const % 2

    def lap(self):
        return self.const // 2 if self.loop is None else self.loop + self.const // 2

    def made(self, eng, sem, per=1, n=None):
        eng.wait_ge(sem, self.t * per + (per if n is None else n))

    def before(self, eng, sem, back, per=1, n=None):
        if self.const >= back:
            eng.wait_ge(sem, (self.t - back) * per + (per if n is None else n))
        else:
            assert self.loop is None


class Pair(Tile):

    def __init__(self, loop, const):
        self.loop, self.const = loop, const // 2
        self.t = const // 2 if loop is None else loop + const // 2


def steps(eng, body, tiles, depth, first):
    assert first >= depth and (tiles - first) % 2 == 0

    def at(loop, const):
        def tile_at(lag):
            c = const - lag
            if loop is None and not 0 <= c < tiles:
                return None
            return Tile(loop, c)
        return tile_at

    for j in range(first):
        body(at(None, j))
    with eng.Fori(0, (tiles - first) // 2) as i:
        for u in range(2):
            body(at(i, first + u))
    for j in range(tiles, tiles + depth):
        body(at(None, j))


def settle(eng, sem):
    eng.sem_inc(sem, 1)


def bc(ap, shape):
    return ap.to_broadcast(shape)


class Kernel:
    def __init__(self, nc, ctx, io, out):
        self.nc, self.ctx, self.io, self.out = nc, ctx, io, out
        self.S = Sems(nc)

    def sb(self, name, shape, dt, ctx=None):
        return (ctx or self.ctx).enter_context(self.nc.sbuf_tensor(name, shape, dt))



def allocate(k):
    nc, sb = k.nc, k.sb
    k.psum = k.ctx.enter_context(nc.psum_tensor("psum", [P, 8, 512], F32))
    k.bank = [k.psum[:, i] for i in range(8)]
    k.h = sb("residual", [P, TILES, D], F32)
    k.ident = sb("ident", [P, P], F32)
    k.ident_bf = sb("ident_bf", [P, P], BF16)
    k.causal = sb("causal", [P, P], BF16)
    k.before = sb("before", [P, P], BF16)
    k.ones_bf = sb("ones_bf", [P, P], BF16)
    k.zeros = sb("zeros", [P, D], F32)
    k.nhalf = sb("nhalf", [P, 1], F32)
    k.parity = sb("parity", [P, 2], F32)
    k.parity_i = sb("parity_i", [P, 2], I32)
    k.iota_e = sb("iota_e", [P, E0], F32)
    k.pidx = sb("pidx", [P, 1], F32)
    k.trash0 = sb("trash0", [P, 1], F32)
    k.trash1 = sb("trash1", [P, 1], F32)
    k.ids = sb("ids", [P, TILES], U32)
    k.stats = sb("stats", [P, 2, 6], F32)
    k.agg = sb("agg", [P, 2, 2], F32)
    k.eps = sb("eps", [P, 2], F32)
    k.mv = sb("mv", [P, TILES, 2], F32)
    k.rstd = sb("rstd", [P, TILES], F32)
    k.wqkv = sb("wqkv", [P, 3, KD, D], F32)
    k.wqkv1 = sb("wqkv1", [P, 3, KD, D], F32)
    k.bqk = sb("bqk", [P, 2, 2], F32)
    k.bv = sb("bv", [P, D], F32)
    k.gate = sb("gate", [P, KD, E0], F32)
    k.gate_bf = sb("gate_bf", [P, KD, E0], BF16)
    k.bias = sb("bias", [P, E0], F32)
    k.router = sb("router", [P, KD, E1], F32)
    k.count0 = sb("count0", [P, 2, E0], BF16)
    k.count1 = sb("count1", [P, E1], BF16)
    k.first_ctx = ExitStack()
    k.zhi, k.zlo = (sb(n, [P, KD, TOKENS], F32R, k.first_ctx) for n in ("zhi", "zlo"))
    k.table0 = nc.dram_tensor("table0", (E0 * CAP0 + P, 2), U32).ap()
    k.table1 = nc.dram_tensor("table1", (E1 * STRIDE1 + P, 2), U32).ap()
    k.z0 = nc.dram_tensor("z0", (TOKENS + PAD0, D), F32).ap()
    k.z1 = nc.dram_tensor("z1", (TOKENS + PAD, D), F32).ap()
    k.acc = nc.dram_tensor("acc", (TOKENS + PAD0, D), F32).ap()


def setup(k):
    nc, S, io = k.nc, k.S, k.io
    n0, n1 = (E0 * CAP0 + P) // P, (E1 * STRIDE1 + P) // P
    with ExitStack() as ctx:
        rows0 = k.sb("rows0", [P, n0], I32, ctx)
        rows1 = k.sb("rows1", [P, n1], I32, ctx)
        low0 = k.sb("low0", [P, n0], I32, ctx)
        low1 = k.sb("low1", [P, n1], I32, ctx)
        init0 = k.sb("init0", [P, n0, 2], U32, ctx)
        init1 = k.sb("init1", [P, n1, 2], U32, ctx)
        rowi = k.sb("rowi", [P, 2], I32, ctx)
        block = ctx.enter_context(nc.Block())

        @block.sync
        def _(sp):
            def zeros(rows, sem):
                view = rows.rearrange("(c p) d -> p c d", p=P)
                sp.dma_start(view, bc(k.zeros[:].unsqueeze(1), view.shape)).then_inc(S(sem), 16)
            for q in range(4):
                sp.dma_start(k.h[:, 4 * q:4 * q + 4, :],
                             io["x"][4 * q:4 * q + 4, ::2, :].rearrange("t p d -> p t d")).then_inc(S("x_loaded"), 16)
            sp.wait_ge(S("init_made"), 4)
            sp.dma_start(k.table0.rearrange("(p c) w -> p (c w)", p=P),
                         init0[:].rearrange("p c w -> p (c w)")).then_inc(S("tables_set"), 16)
            sp.dma_start(k.table1.rearrange("(p c) w -> p (c w)", p=P),
                         init1[:].rearrange("p c w -> p (c w)")).then_inc(S("tables_set"), 16)
            sp.wait_ge(S("zeros_made"), 1)
            zeros(k.z0[TOKENS:, :], "pads_set")
            zeros(k.z1[TOKENS:, :], "pads_set")
            zeros(k.out[TOKENS:, :], "pads_set")
            zeros(k.acc, "acc_set")
            sp.wait_ge(S("tables_set"), 32)
            sp.wait_ge(S("pads_set"), 48)
            sp.wait_ge(S("acc_set"), 16)
            sp.wait_ge(S("x_loaded"), 64)

        @block.scalar
        def _(act):
            act.dma_start(k.wqkv[:], io["wqkv"]).then_inc(S("weights_loaded"), 16)
            act.dma_start(k.bqk[:], io["bqk"]).then_inc(S("weights_loaded"), 16)
            act.dma_start(k.bv[:], io["bv"].partition_broadcast(P)).then_inc(S("weights_loaded"), 16)
            act.dma_start(k.gate_bf[:], io["gate"]).then_inc(S("weights_loaded"), 16)
            act.dma_start(k.bias[:], io["bias"].partition_broadcast(P)).then_inc(S("weights_loaded"), 16)
            act.dma_start(k.router[:], io["router"]).then_inc(S("weights_loaded"), 16)
            act.dma_start(k.wqkv1[:], io["wqkv1"]).then_inc(S("weights_loaded"), 16)
            act.wait_ge(S("weights_loaded"), 112)

        @block.gpsimd
        def _(pool):
            pool.memset(k.ident[:], 0.0).then_inc(S("filled"), 1)
            pool.memset(k.causal[:], 0.0).then_inc(S("filled"), 1)
            pool.memset(k.ones_bf[:], 1.0).then_inc(S("filled"), 1)
            pool.memset(k.zeros[:], 0.0).then_inc(S("zeros_made"), 1)
            pool.memset(k.nhalf[:], -0.5)
            pool.memset(k.eps[:, 0:1], 0.0)
            pool.memset(k.eps[:, 1:2], EPS)
            pool.wait_ge(S("filled"), 3)
            pool.affine_select(out=k.ident[:], in_=k.ident[:], compare_op=ALU.not_equal, fill=1.0, base=0,
                               pattern=[[-1, P]], channel_multiplier=1).then_inc(S("ident_made"), 1)
            pool.affine_select(out=k.causal[:], in_=k.causal[:], compare_op=ALU.is_ge, fill=MASKED, base=0,
                               pattern=[[-1, P]], channel_multiplier=1)
            pool.affine_select(out=k.before[:], in_=k.ones_bf[:], compare_op=ALU.is_gt, fill=0.0, base=0,
                               pattern=[[1, P]], channel_multiplier=-1)
            pool.iota(k.ids[:], pattern=[[P, TILES]], base=0, channel_multiplier=1)
            pool.iota(rowi[:], pattern=[[0, 2]], base=0, channel_multiplier=1).then_inc(S("iotas"), 1)
            pool.iota(rows0[:], pattern=[[1, n0]], base=0, channel_multiplier=n0).then_inc(S("iotas"), 1)
            pool.iota(rows1[:], pattern=[[1, n1]], base=0, channel_multiplier=n1).then_inc(S("iotas"), 1)
            for out, base, step, mult in ((k.iota_e, 0, 1, 0), (k.pidx, 0, 0, 1), (k.trash0, E0 * CAP0, 0, 1),
                                          (k.trash1, E1 * STRIDE1, 0, 1)):
                pool.iota(out[:], pattern=[[step, out.shape[1]]], base=base, channel_multiplier=mult,
                          allow_small_or_imprecise_dtypes=True)

        @block.vector
        def _(dve):
            dve.wait_ge(S("iotas"), 3)
            dve.memset(init0[:].bitcast(F32), 0.0).then_inc(S("init_zero"), 1)
            dve.memset(init1[:].bitcast(F32), 0.0).then_inc(S("init_zero"), 1)
            dve.tensor_scalar(low0[:], rows0[:], PAD0 - 1, None, ALU.bitwise_and).then_inc(S("low_made"), 1)
            dve.tensor_scalar(low1[:], rows1[:], PAD - 1, None, ALU.bitwise_and).then_inc(S("low_made"), 1)
            dve.tensor_scalar(k.parity_i[:], rowi[:], 4, 1, ALU.logical_shift_right,
                              ALU.bitwise_and).then_inc(S("low_made"), 1)
            dve.wait_ge(S("init_zero"), 2)
            dve.wait_ge(S("low_made"), 3)
            dve.tensor_scalar(init0[:, :, 0], low0[:], float(TOKENS), None, ALU.add).then_inc(S("init_made"), 1)
            dve.tensor_scalar(init1[:, :, 0], low1[:], float(TOKENS), None, ALU.add).then_inc(S("init_made"), 1)
            dve.tensor_scalar(k.parity[:, 0:1], k.parity_i[:, 0:1], -1.0, 1.0, ALU.mult, ALU.add).then_inc(S("init_made"), 1)
            dve.tensor_copy(k.parity[:, 1:2], k.parity_i[:, 1:2]).then_inc(S("init_made"), 1)
            dve.wait_ge(S("ident_made"), 1)
            dve.tensor_copy(k.ident_bf[:], k.ident[:])
            dve.wait_ge(S("weights_loaded"), 112)
            dve.tensor_copy(k.gate[:], k.gate_bf[:])


def token_attention(k):
    nc, S = k.nc, k.S
    with ExitStack() as ctx:
        sb = lambda n, s, d: k.sb("ta_" + n, s, d, ctx)
        bank = k.bank
        xin, xT = sb("xin", [P, 2, D], F32), sb("xT", [P, 2, KD, P], F32)
        mx, shift = sb("mx", [P, 2], F32), sb("shift", [P, 2], F32)
        probs, total, recip = sb("probs", [P, 2, P], F32), sb("total", [P, 2], F32), sb("recip", [P, 2], F32)
        pT = sb("pT", [P, 2, P], F32)
        scale = D ** -0.5
        block = ctx.enter_context(nc.Block())
        DEPTH, FIRST = 3, 6

        @block.sync
        def _(sp):
            def body(at):
                if t := at(0):
                    t.before(sp, S("ta_xT_turned"), 2)
                    sp.dma_start(xin[:, t.par], k.io["x"][t.t, ::2, :]).then_inc(S(f"ta_xin{t.par}"), 16)
            steps(sp, body, TILES, DEPTH, FIRST)

        @block.tensor
        def _(pe):
            def body(at):
                if t := at(0):
                    pe.wait_ge(S(f"ta_xin{t.par}"), t.lap() * 16 + 16)
                    t.before(pe, S("ta_xT"), 2)
                    for c in range(KD):
                        mm = pe.transpose(bank[t.par][:, c * P:(c + 1) * P], xin[:, t.par, c * P:(c + 1) * P], k.ident[:])
                    mm.then_inc(S("ta_xT_turned"), 1)
                if t := at(1):
                    t.made(pe, S("ta_xT"))
                    t.before(pe, S("ta_probs"), 2)
                    for c in range(KD):
                        mm = pe.matmul(bank[2 + t.par][:, 0:P], xT[:, t.par, c], xT[:, t.par, c], start=c == 0, stop=c == KD - 1)
                    mm.then_inc(S("ta_scores"), 1)
                if t := at(2):
                    t.made(pe, S("ta_probs"))
                    t.before(pe, S("ta_pT"), 2)
                    pe.transpose(bank[4 + t.par][:, 0:P], probs[:, t.par], k.ident[:]).then_inc(S("ta_pT_turned"), 1)
                if t := at(3):
                    t.made(pe, S("ta_pT"))
                    t.before(pe, S("ta_h"), 2)
                    pe.matmul(bank[6 + t.par][:, 0:D], pT[:, t.par], k.h[:, t.t, :], start=True, stop=True).then_inc(S("ta_out"), 1)
            steps(pe, body, TILES, DEPTH, FIRST)

        @block.scalar
        def _(act):
            act.preload_act_table(ACT.Exp)

            def body(at):
                if t := at(0):
                    t.made(act, S("ta_xT_turned"))
                    t.before(act, S("ta_scores"), 2)
                    act.copy(xT[:, t.par].rearrange("p c q -> p (c q)"), bank[t.par][:, 0:D]).then_inc(S("ta_xT"), 1)
                if t := at(1):
                    t.made(act, S("ta_shift"))
                    t.before(act, S("ta_pT_turned"), 2)
                    act.activation(probs[:, t.par], bank[2 + t.par][:, 0:P], ACT.Exp, bias=shift[:, t.par:t.par + 1],
                                   scale=scale, accum_out=total[:, t.par:t.par + 1]).then_inc(S("ta_probs"), 1)
            steps(act, body, TILES, DEPTH, FIRST)

        @block.vector
        def _(dve):
            def body(at):
                if t := at(3):
                    t.made(dve, S("ta_probs"))
                    t.before(dve, S("ta_h"), 2)
                    dve.reciprocal(recip[:, t.par:t.par + 1], total[:, t.par:t.par + 1]).then_inc(S("ta_recip"), 1)
                if t := at(1):
                    t.made(dve, S("ta_scores"))
                    t.before(dve, S("ta_shift"), 2)
                    dve.tensor_reduce(mx[:, t.par:t.par + 1], bank[2 + t.par][:, 0:P], AX.X, ALU.max).then_inc(S("ta_max"), 1)
                if t := at(3):
                    t.made(dve, S("ta_recip"))
                    t.made(dve, S("ta_out"))
                    dve.tensor_scalar(k.h[:, t.t, :], bank[6 + t.par][:, 0:D], recip[:, t.par:t.par + 1], None,
                                      ALU.mult).then_inc(S("ta_h"), 1)
                if t := at(1):
                    t.made(dve, S("ta_max"))
                    t.before(dve, S("ta_probs"), 2)
                    dve.tensor_scalar(shift[:, t.par:t.par + 1], mx[:, t.par:t.par + 1], -scale, None,
                                      ALU.mult).then_inc(S("ta_shift"), 1)
                if t := at(3):
                    t.made(dve, S("ta_h"))
                    settle(dve, S("settled_dve"))
                    dve.bn_stats(k.stats[:, t.par], k.h[:, t.t, :]).then_inc(S("ta_stats"), 1)
                if t := at(2):
                    t.made(dve, S("ta_pT_turned"))
                    t.before(dve, S("ta_out"), 2)
                    dve.tensor_copy(pT[:, t.par], bank[4 + t.par][:, 0:P]).then_inc(S("ta_pT"), 1)
                if t := at(3):
                    t.made(dve, S("ta_stats"))
                    settle(dve, S("settled_dve"))
                    dve.bn_aggr(k.agg[:, t.par], k.stats[:, t.par]).then_inc(S("ta_mv"), 1)
                    t.made(dve, S("ta_mv"))
                    dve.tensor_tensor(k.mv[:, t.t, :], k.agg[:, t.par], k.eps[:], ALU.add).then_inc(S("ta_ve"), 1)
            steps(dve, body, TILES, DEPTH, FIRST)

        @block.gpsimd
        def _(pool):
            with pool.Fori(0, TILES) as t:
                pool.wait_ge(S("ta_ve"), t + 1)
                pool.tensor_tensor(k.rstd[:, bass.ds(t, 1)], k.mv[:, t, 1:2], k.nhalf[:], ALU.pow)


def head_attention(k):
    nc, S = k.nc, k.S
    with ExitStack() as ctx:
        sb = lambda n, s, d: k.sb("ha_" + n, s, d, ctx)
        bank = k.bank
        z, zT = sb("z", [P, 2, D], F32), sb("zT", [P, 2, KD, P], F32)
        q = [sb(f"q{o}", [P, 2, 2, P], F32) for o in range(2)]
        kT = sb("kT", [P, 2, 2, P], F32)
        v = sb("v", [P, 2, HEADS, HEAD + 1], F32)
        bqm = sb("bqm", [P, 2, 2], F32)
        mx = sb("mx", [P, 2, HEADS], F32)
        probs = sb("probs", [P, 2, HEADS * P], F32)
        pT = sb("pT", [P, GROUPS, 4 * P], F32)
        recip, o = sb("recip", [P, 2, HEADS, 1], F32), sb("o", [P, 2, D], F32)
        z2, z2T = sb("z2", [P, 2, D], F32), sb("z2T", [P, 2, KD, P], F32)
        eg, s1 = sb("eg", [P, 2, E0], F32), sb("s1", [P, 2, E0], F32)
        gate, biased = sb("gate", [P, 2, E0], F32), sb("biased", [P, 2, E0], F32)
        top, topi = sb("top", [P, 2, 8], F32), sb("topi", [P, 2, 8], U32)
        choice = sb("choice", [P, 2, K0], F32)
        onehot, picked = sb("onehot", [P, 2, K0, E0], F32), sb("picked", [P, 2, K0, E0], F32)
        ranked = sb("ranked", [P, 2, K0, E0], F32)
        chosen = sb("chosen", [P, 2, E0], BF16)
        w, wsum, wr = sb("w", [P, 2, K0], F32), sb("wsum", [P, 2, 2], F32), sb("wr", [P, 2, 1], F32)
        rank, kept = sb("rank", [P, 2, K0], F32), sb("kept", [P, 2, K0], F32)
        slot, slot2 = sb("slot", [P, 2, K0], F32), sb("slot2", [P, 2, K0], F32)
        to = sb("to", [P, 2, K0], U32)
        pay = sb("pay", [P, 2, K0, 2], U32)
        B_ZT, B_Q, B_S, B_PT, B_O, B_KV = 0, 1, 2, 4, 6, 7
        DEPTH, FIRST = 4, 6
        scale = HEAD ** -0.5
        wq, wk, wv = (k.wqkv[:, n] for n in range(3))
        block = ctx.enter_context(nc.Block())

        @block.tensor
        def _(pe):
            def scores(t, g):
                b = bank[B_S + g % 2]
                if g >= 2:
                    t.made(pe, S("ha_centred"), 4, g - 1)
                else:
                    t.before(pe, S("ha_centred"), 1, 4, g + 3)
                if g == 0:
                    t.made(pe, S("ha_q"), 2)
                    t.made(pe, S("ha_k"), 2)
                rows = slice(32 * g, 32 * g + 32)
                for n in range(4):
                    mm = pe.matmul(b[:, n * P:(n + 1) * P], q[n % 2][rows, t.par, n // 2], kT[rows, t.par, n // 2],
                                   start=n == 0, stop=False, skip_group_check=True)
                mm = pe.matmul(b[:].rearrange("p (n q) -> p n q", n=4), k.ident_bf[:], bc(k.causal[:].unsqueeze(1), [P, 4, P]),
                               start=False, stop=True, skip_group_check=True)
                mm.then_inc(S("ha_scores"), 1)

            def turn_probs(t, g):
                t.made(pe, S("ha_probs"), 4, g + 1)
                if g >= 2:
                    t.made(pe, S("ha_pT"), 4, g - 1)
                else:
                    t.before(pe, S("ha_pT"), 1, 4, g + 3)
                for n in range(4):
                    c = (4 * g + n) * P
                    mm = pe.transpose(bank[B_PT + g % 2][:, n * P:(n + 1) * P], probs[:, t.par, c:c + P], k.ident[:])
                mm.then_inc(S("ha_pT_turned"), 1)

            def weigh(t, g):
                t.made(pe, S("ha_pT"), 4, g + 1)
                if g == 0:
                    t.made(pe, S("ha_v"))
                    t.before(pe, S("ha_o"), 1)
                for n in range(4):
                    head = 8 * (n // 2) + 2 * g + n % 2
                    mm = pe.matmul(bank[B_O][:, head * (HEAD + 1):(head + 1) * (HEAD + 1)], pT[:, g, n * P:(n + 1) * P],
                                   v[:, t.par, head], start=True, stop=True)
                mm.then_inc(S("ha_out"), 1)

            def body(at):
                f, s, p, r, w_ = (at(n) for n in range(5))
                if s:
                    scores(s, 0)
                if p:
                    turn_probs(p, 0)
                if f:
                    f.made(pe, S("ha_z"))
                    f.before(pe, S("ha_zT"), 1)
                    f.before(pe, S("r0_hi"), 4)
                    for c in range(KD):
                        mm = pe.transpose(bank[B_ZT][:, c * P:(c + 1) * P], z[:, f.par, c * P:(c + 1) * P], k.ident[:])
                    mm.then_inc(S("ha_zT_turned"), 1)
                if s:
                    scores(s, 1)
                if p:
                    turn_probs(p, 1)
                if r:
                    r.made(pe, S("r0_z2"))
                    r.before(pe, S("r0_hi"), 1)
                    if f:
                        f.made(pe, S("ha_zT"))
                    for c in range(KD):
                        mm = pe.transpose(bank[B_ZT][:, c * P:(c + 1) * P], z2[:, r.par, c * P:(c + 1) * P], k.ident[:])
                    mm.then_inc(S("r0_z2T_turned"), 1)
                if p:
                    weigh(p, 0)
                if f:
                    f.made(pe, S("ha_zT"))
                    f.before(pe, S("ha_q"), 1, 2)
                    if w_:
                        w_.made(pe, S("r0_ranked"))
                    for c in range(2):
                        for d in range(KD):
                            mm = pe.matmul(bank[B_Q][:, c * P:(c + 1) * P], wq[:, d, c * P:(c + 1) * P], zT[:, f.par, d],
                                           start=d == 0, stop=d == KD - 1)
                    mm.then_inc(S("ha_q_projected"), 1)
                if s:
                    scores(s, 2)
                if p:
                    turn_probs(p, 2)
                    weigh(p, 1)
                if f:
                    f.before(pe, S("ha_v"), 1)
                    for c in range(2):
                        for d in range(KD):
                            pe.matmul(bank[B_KV][:, c * P:(c + 1) * P], wk[:, d, c * P:(c + 1) * P], zT[:, f.par, d],
                                      start=d == 0, stop=d == KD - 1)
                    for d in range(KD):
                        mm = pe.matmul(bank[B_KV][:, D:2 * D], zT[:, f.par, d], wv[:, d], start=d == 0, stop=d == KD - 1)
                    mm.then_inc(S("ha_kv_projected"), 1)
                if r:
                    r.made(pe, S("r0_z2T"))
                    if w_:
                        w_.made(pe, S("r0_ranked"))
                    if f:
                        f.made(pe, S("ha_q"), 2)
                    for d in range(KD):
                        mm = pe.matmul(bank[B_Q][:, D:D + E0], z2T[:, r.par, d], k.gate[:, d], start=d == 0, stop=d == KD - 1)
                    mm.then_inc(S("r0_logits"), 1)
                if s:
                    scores(s, 3)
                if p:
                    turn_probs(p, 3)
                    weigh(p, 2)
                    weigh(p, 3)
                if r:
                    r.made(pe, S("r0_chosen"))
                    r.before(pe, S("r0_counted"), 1)
                    pe.matmul(bank[B_Q][:, 2 * E0 + D:3 * E0 + D], k.before[:], chosen[:, r.par], start=True, stop=False)
                    pe.matmul(bank[B_Q][:, 2 * E0 + D:3 * E0 + D], k.ones_bf[:], k.count0[:, r.par],
                              start=False, stop=True).then_inc(S("r0_ranks"), 1)
            steps(pe, body, TILES, DEPTH, FIRST)

        @block.scalar
        def _(act):
            act.preload_act_table(ACT.Exp)

            def copy_probs(t, g):
                t.made(act, S("ha_pT_turned"), 4, g + 1)
                t.before(act, S("ha_out"), 1, 4, g + 1)
                act.copy(pT[:, g], bank[B_PT + g % 2][:]).then_inc(S("ha_pT"), 1)

            def exponentials(t, g):
                c = slice(4 * g * P, 4 * (g + 1) * P)
                t.made(act, S("ha_centred"), 4, g + 1)
                act.activation(probs[:, t.par, c], probs[:, t.par, c], ACT.Exp, scale=scale).then_inc(S("ha_probs"), 1)

            def body(at):
                f, s, p, r = (at(n) for n in range(4))
                if p:
                    copy_probs(p, 0)
                if s:
                    exponentials(s, 0)
                if f:
                    f.made(act, S("ha_zT_turned"))
                    f.before(act, S("ha_kv_projected"), 2)
                    act.copy(zT[:, f.par].rearrange("p c q -> p (c q)"), bank[B_ZT][:, 0:D]).then_inc(S("ha_zT"), 1)
                if p:
                    copy_probs(p, 1)
                if s:
                    exponentials(s, 1)
                if r:
                    r.made(act, S("r0_z2T_turned"))
                    r.before(act, S("r0_lo"), 2)
                    act.copy(z2T[:, r.par].rearrange("p c q -> p (c q)"), bank[B_ZT][:, 0:D]).then_inc(S("r0_z2T"), 1)
                    act.copy(k.zhi[:, :, bass.ts(r.t, P)], bank[B_ZT][:, 0:D].rearrange("p (c q) -> p c q", c=KD)
                             ).then_inc(S("r0_hi"), 1)
                if p:
                    copy_probs(p, 2)
                if s:
                    exponentials(s, 2)
                if f:
                    f.made(act, S("ha_kv_projected"))
                    f.before(act, S("ha_scores"), 2, 4)
                    for c in range(2):
                        act.activation(kT[:, f.par, c], bank[B_KV][:, c * P:(c + 1) * P], ACT.Identity,
                                       bias=k.bqk[:, 1, c:c + 1]).then_inc(S("ha_k"), 1)
                if r:
                    r.made(act, S("r0_logits"))
                    r.before(act, S("r0_s1"), 2)
                    act.activation(eg[:, r.par], bank[B_Q][:, D:D + E0], ACT.Exp, scale=-1.0).then_inc(S("r0_eg"), 1)
                if p:
                    copy_probs(p, 3)
                if s:
                    exponentials(s, 3)
                if f:
                    f.before(act, S("ha_out"), 2, 4)
                    act.copy(v[:, f.par, :, 0:HEAD], bank[B_KV][:, D:2 * D].rearrange("p (h e) -> p h e", h=HEADS)
                             ).then_inc(S("ha_v"), 1)
            steps(act, body, TILES, DEPTH, FIRST)

        @block.vector
        def _(dve):
            for par in range(2):
                dve.memset(v[:, par, :, HEAD:HEAD + 1], 1.0)
                for c in range(2):
                    dve.tensor_scalar(bqm[:, par, c:c + 1], k.bqk[:, 0, c:c + 1], k.parity[:, par:par + 1], None, ALU.mult)
            dve.memset(k.count0[:, 0], 0.0).then_inc(S("ha_set"), 1)
            dve.wait_ge(S("ha_set"), 1)

            def centre(t, g):
                c = 4 * g
                view = bank[B_S + g % 2][:].rearrange("p (n q) -> p n q", n=4)
                t.made(dve, S("ha_scores"), 4, g + 1)
                t.before(dve, S("ha_centred"), 2, 4, g + 1)
                dve.tensor_reduce(mx[:, t.par, c:c + 4], view, AX.X, ALU.max).then_inc(S("ha_max"), 1)
                yield
                t.made(dve, S("ha_max"), 4, g + 1)
                t.before(dve, S("ha_pT_turned"), 2, 4, g + 1)
                dve.tensor_tensor(probs[:, t.par, c * P:(c + 4) * P].rearrange("p (n q) -> p n q", n=4), view,
                                  bc(mx[:, t.par, c:c + 4].unsqueeze(2), [P, 4, P]), ALU.subtract
                                  ).then_inc(S("ha_centred"), 1)
                yield

            def route(r):
                r.made(dve, S("r0_eg"))
                dve.tensor_scalar(s1[:, r.par], eg[:, r.par], 1.0, None, ALU.add).then_inc(S("r0_s1"), 1)
                yield
                r.made(dve, S("r0_s1"))
                dve.reciprocal(gate[:, r.par], s1[:, r.par]).then_inc(S("r0_gate"), 1)
                yield
                r.made(dve, S("r0_gate"))
                dve.tensor_tensor(biased[:, r.par], gate[:, r.par], k.bias[:], ALU.add).then_inc(S("r0_biased"), 1)
                yield
                r.made(dve, S("r0_biased"))
                settle(dve, S("settled_dve"))
                dve.max(top[:, r.par], biased[:, r.par]).then_inc(S("r0_top"), 1)
                yield
                r.made(dve, S("r0_top"))
                settle(dve, S("settled_dve"))
                dve.max_index(topi[:, r.par], top[:, r.par], biased[:, r.par]).then_inc(S("r0_topi"), 1)
                yield
                r.made(dve, S("r0_topi"))
                dve.tensor_copy(choice[:, r.par], topi[:, r.par, 0:K0]).then_inc(S("r0_choice"), 1)
                yield
                r.made(dve, S("r0_choice"))
                dve.tensor_tensor(onehot[:, r.par], bc(k.iota_e[:].unsqueeze(1), [P, K0, E0]),
                                  bc(choice[:, r.par].unsqueeze(2), [P, K0, E0]), ALU.is_equal).then_inc(S("r0_onehot"), 1)
                yield
                r.made(dve, S("r0_onehot"))
                with nc.allow_low_precision("counts of 0 and 1"):
                    dve.tensor_reduce(chosen[:, r.par], onehot[:, r.par].rearrange("p n e -> p e n"), AX.X,
                                      ALU.add).then_inc(S("r0_chosen"), 1)
                yield

            def weights(w_):
                par = w_.par
                w_.made(dve, S("r0_ranks"))
                dve.tensor_tensor(ranked[:, par], onehot[:, par],
                                  bc(bank[B_Q][:, 2 * E0 + D:3 * E0 + D].unsqueeze(1), [P, K0, E0]), ALU.mult
                                  ).then_inc(S("r0_ranked"), 1)
                dve.tensor_tensor(picked[:, par], onehot[:, par], bc(gate[:, par].unsqueeze(1), [P, K0, E0]), ALU.mult
                                  ).then_inc(S("r0_picked"), 1)
                dve.tensor_tensor(k.count0[:, 1 - par], k.count0[:, par], chosen[:, par], ALU.add).then_inc(S("r0_counted"), 1)
                yield
                w_.made(dve, S("r0_ranked"))
                dve.tensor_reduce(rank[:, par], ranked[:, par], AX.X, ALU.add).then_inc(S("r0_rank"), 1)
                w_.made(dve, S("r0_picked"))
                dve.tensor_reduce(w[:, par], picked[:, par], AX.X, ALU.add).then_inc(S("r0_w"), 1)
                yield
                w_.made(dve, S("r0_rank"))
                dve.tensor_scalar(kept[:, par], rank[:, par], float(CAP0), None, ALU.is_lt).then_inc(S("r0_kept"), 1)
                dve.scalar_tensor_tensor(slot[:, par], choice[:, par], float(CAP0), rank[:, par], ALU.mult, ALU.add
                                         ).then_inc(S("r0_slot"), 1)
                w_.made(dve, S("r0_w"))
                dve.tensor_reduce(wsum[:, par, 0:1], w[:, par], AX.X, ALU.add).then_inc(S("r0_wsum"), 1)
                yield
                w_.made(dve, S("r0_slot"))
                w_.made(dve, S("r0_kept"))
                dve.scalar_tensor_tensor(slot2[:, par], slot[:, par], k.trash0[:, 0:1], kept[:, par], ALU.subtract,
                                         ALU.mult).then_inc(S("r0_slot2"), 1)
                w_.made(dve, S("r0_wsum"))
                dve.tensor_scalar(wsum[:, par, 1:2], wsum[:, par, 0:1], 1e-12, None, ALU.max).then_inc(S("r0_clipped"), 1)
                yield
                w_.made(dve, S("r0_slot2"))
                if w_.const >= 2:
                    dve.wait_ge(S(f"r0_scattered{par}"), w_.lap() * 16 * K0)
                dve.tensor_scalar(to[:, par], slot2[:, par], k.trash0[:, 0:1], None, ALU.add).then_inc(S("r0_to"), 1)
                w_.made(dve, S("r0_clipped"))
                dve.reciprocal(wr[:, par], wsum[:, par, 1:2]).then_inc(S("r0_wr"), 1)
                dve.tensor_copy(pay[:, par, :, 0], bc(k.ids[:, bass.ds(w_.t, 1)], [P, K0])).then_inc(S("r0_pay"), 1)
                yield
                w_.made(dve, S("r0_wr"))
                dve.scalar_tensor_tensor(pay[:, par, :, 1].bitcast(F32), w[:, par], wr[:, par], kept[:, par], ALU.mult,
                                         ALU.mult).then_inc(S("r0_pay"), 1)
                yield

            def body(at):
                f, s, p, r, w_ = (at(n) for n in range(5))
                small = iter(())
                if f:
                    f.before(dve, S("ha_zT_turned"), 2)
                    dve.tensor_scalar(z[:, f.par], k.h[:, f.t, :], k.mv[:, f.t, 0:1], k.rstd[:, bass.ds(f.t, 1)],
                                      ALU.subtract, ALU.mult).then_inc(S("ha_z"), 1)
                if r:
                    r.made(dve, S("ha_rstd"))
                    if r.const >= 2:
                        dve.wait_ge(S(f"r0_stored{r.par}"), r.lap() * 16)
                    dve.tensor_scalar(z2[:, r.par], k.h[:, r.t, :], k.mv[:, r.t, 0:1], k.rstd[:, bass.ds(r.t, 1)],
                                      ALU.subtract, ALU.mult).then_inc(S("r0_z2"), 1)
                if w_:
                    small = weights(w_)
                for g in range(4):
                    if s:
                        for _ in centre(s, g):
                            next(small, None)
                            next(small, None)
                    elif g < 2:
                        for _ in range(4):
                            next(small, None)
                    if g == 1:
                        for _ in small:
                            pass
                        if f:
                            f.made(dve, S("ha_q_projected"))
                            f.before(dve, S("ha_scores"), 2, 4)
                            for o_ in range(2):
                                dve.scalar_tensor_tensor(q[o_][:, f.par], bank[B_Q][:, 0:D].rearrange("p (c q) -> p c q", c=2),
                                                         k.parity[:, o_:o_ + 1],
                                                         bc(bqm[:, o_].unsqueeze(2), [P, 2, P]), ALU.mult, ALU.add
                                                         ).then_inc(S("ha_q"), 1)
                        if r:
                            r.made(dve, S("r0_hi"))
                            dve.tensor_tensor(k.zlo[:, :, bass.ts(r.t, P)], z2T[:, r.par],
                                              k.zhi[:, :, bass.ts(r.t, P)].bitcast(F32), ALU.subtract
                                              ).then_inc(S("r0_lo"), 1)
                    if g == 2 and r:
                        small = route(r)
                for _ in small:
                    pass
                if p:
                    norm(p)

            def norm(p):
                par = p.par
                view = bank[B_O][:, 0:HEADS * (HEAD + 1)].rearrange("p (h e) -> p h e", h=HEADS)
                p.made(dve, S("ha_out"), 4)
                dve.reciprocal(recip[:, par], view[:, :, HEAD:HEAD + 1]).then_inc(S("ha_recip"), 1)
                p.made(dve, S("ha_recip"))
                dve.tensor_tensor(o[:, par].rearrange("p (h e) -> p h e", h=HEADS), view[:, :, 0:HEAD],
                                  bc(recip[:, par], [P, HEADS, HEAD]), ALU.mult).then_inc(S("ha_o"), 1)
                p.made(dve, S("ha_o"))
                p.made(dve, S("ha_bv"))
                dve.tensor_tensor(k.h[:, p.t, :], k.h[:, p.t, :], o[:, par], ALU.add).then_inc(S("ha_h"), 1)
                p.made(dve, S("ha_h"))
                settle(dve, S("settled_dve"))
                dve.bn_stats(k.stats[:, par], k.h[:, p.t, :]).then_inc(S("ha_stats"), 1)
                p.made(dve, S("ha_stats"))
                settle(dve, S("settled_dve"))
                dve.bn_aggr(k.agg[:, par], k.stats[:, par]).then_inc(S("ha_mv"), 1)
                p.made(dve, S("ha_mv"))
                dve.tensor_tensor(k.mv[:, p.t, :], k.agg[:, par], k.eps[:], ALU.add).then_inc(S("ha_ve"), 1)
            steps(dve, body, TILES, DEPTH, FIRST)

        @block.gpsimd
        def _(pool):
            def body(at):
                f, p, w_ = at(0), at(2), at(4)
                if f:
                    f.made(pool, S("ha_z"))
                    pool.tensor_tensor(k.h[:, f.t, :], k.h[:, f.t, :], k.bv[:], ALU.add).then_inc(S("ha_bv"), 1)
                if w_:
                    w_.made(pool, S("r0_to"))
                    w_.made(pool, S("r0_pay"), 2)
                    settle(pool, S("settled_pool"))
                    for n in range(K0):
                        pool.indirect_dma_start(out=k.table0, out_offset=bass.IndirectOffsetOnAxis(ap=to[:, w_.par, n:n + 1], axis=0),
                                                in_=pay[:, w_.par, n, :], in_offset=None, bounds_check=E0 * CAP0 - 1,
                                                oob_is_err=False).then_inc(S(f"r0_scattered{w_.par}"), 16)
                if p:
                    p.made(pool, S("ha_ve"))
                    pool.tensor_tensor(k.rstd[:, bass.ds(p.t, 1)], k.mv[:, p.t, 1:2], k.nhalf[:], ALU.pow
                                       ).then_inc(S("ha_rstd"), 1)
            steps(pool, body, TILES, DEPTH, FIRST)
            for par in range(2):
                pool.wait_ge(S(f"r0_scattered{par}"), 16 * K0 * TILES // 2)

        @block.sync
        def _(sp):
            def body(at):
                if r := at(3):
                    r.made(sp, S("r0_z2"))
                    sp.dma_start(k.z0[bass.ts(r.t, P), :], z2[:, r.par]).then_inc(S(f"r0_stored{r.par}"), 16)
            steps(sp, body, TILES, DEPTH, FIRST)
            for par in range(2):
                sp.wait_ge(S(f"r0_stored{par}"), 16 * TILES // 2)


def first_mixture(k):
    nc, S = k.nc, k.S
    TURN, SC = 4, CAP0 // P
    SG = 512 // P
    with ExitStack() as ctx:
        sb = lambda n, s, d: k.sb("m0_" + n, s, d, ctx)
        bank = k.bank
        shared_bf, shared = sb("shared_bf", [P, 3 * D], BF16), sb("shared", [P, 3 * D], F32R)
        sgs, hfs = sb("sgs", [P, 2, 512], F32), sb("hfs", [P, 2, 512], F32)
        hhs, hls = sb("hhs", [P, 2, 512], F32R), sb("hls", [P, 2, 512], F32R)
        active, upto, idle = sb("active", [P, E0], F32), sb("upto", [P, E0], F32), sb("idle", [P, E0], F32)
        place, place2 = sb("place", [P, E0], F32), sb("place2", [P, E0], F32)
        is_at, named = sb("is_at", [P, E0, E0], F32), sb("named", [P, E0, E0], F32)
        order, turns = sb("order", [P, E0 + TURN], I32), sb("turns", [P, 1], I32)
        up3, up3i, tsh = sb("up3", [P, 1], F32), sb("up3i", [P, 1], I32), sb("zero_e", [P, E0], F32)
        slots = sb("slots", [P, TURN, SC, 2], U32)
        x = sb("x", [P, 2, SC, D], F32)
        raw, wts = sb("raw", [P, 2, 3 * D], BF16), sb("wts", [P, 2, 3 * D], F32R)
        xh, xl = sb("xh", [P, 2, KD, CAP0], F32R), sb("xl", [P, 2, KD, CAP0], F32R)
        sg, hf = sb("sg", [P, 2, CAP0], F32), sb("hf", [P, 2, CAP0], F32)
        hh, hl = sb("hh", [P, 2, CAP0], F32R), sb("hl", [P, 2, CAP0], F32R)
        yw = sb("yw", [P, TURN, SC, D], F32)
        B_X, B_H, B_Y, B_C = 0, 2, 4, 7
        table_rows = k.table0[0:E0 * CAP0, :].rearrange("(e c p) w -> e p c w", e=E0, p=P)
        top_e = E0 - 1
        block = ctx.enter_context(nc.Block())

        def w13(t, n, c):
            return t[..., (2 * n + c) * P:(2 * n + c + 1) * P]

        @block.sync
        def _(sp):
            sp.dma_start(shared_bf[:], k.io["shared"]).then_inc(S("m0_shared_loaded"), 16)
            sp.wait_ge(S("m0_listed"), 2)
            count = sp.value_load(turns[0:1, 0:1], min_val=1, max_val=E0 // TURN)

            def expert(at):
                return sp.value_load(order[0:1, at], min_val=0, max_val=top_e)

            def weights(e, u):
                sp.dma_start(raw[:, u], k.io["moe0"][e]).then_inc(S(f"m0_raw{u}"), 16)

            def table(e, v):
                sp.dma_start(slots[:, v], table_rows[e]).then_inc(S(f"m0_slots{v}"), 16)
            for v in range(TURN):
                e = expert(slice(v, v + 1))
                table(e, v)
                if v < 2:
                    weights(e, v)
            with sp.Fori(0, count) as i:
                for v in range(TURN):
                    m = i * TURN + v
                    sp.wait_ge(S("m0_cast"), m + 1)
                    settle(sp, S("settled_sp"))
                    weights(expert(bass.ds(m + 2, 1)), v % 2)
                    sp.wait_ge(S("m0_added"), (m + 1) * 16 * SC)
                    settle(sp, S("settled_sp"))
                    table(expert(bass.ds(m + TURN, 1)), v)
            for u in range(2):
                sp.wait_ge(S(f"m0_raw{u}"), (count * 2 + 1) * 16)
            for v in range(TURN):
                sp.wait_ge(S(f"m0_slots{v}"), (count + 1) * 16)
            settle(sp, S("settled_sp"))

        @block.gpsimd
        def _(pool):
            pool.wait_ge(S("m0_listed"), 2)
            count = pool.value_load(turns[0:1, 0:1], min_val=1, max_val=E0 // TURN)

            def gather(v, u):
                for c in range(SC):
                    pool.indirect_dma_start(out=x[:, u, c, :], out_offset=None, in_=k.z0,
                                            in_offset=bass.IndirectOffsetOnAxis(ap=slots[:, v, c, 0:1], axis=0)
                                            ).then_inc(S(f"m0_x{u}"), 16)
            for v in range(2):
                pool.wait_ge(S(f"m0_slots{v}"), 16)
                gather(v, v)
            with pool.Fori(0, count) as i:
                for pair in range(TURN // 2):
                    for v in (2 * pair, 2 * pair + 1):
                        m, ahead = i * TURN + v, (v + 2) % TURN
                        pool.wait_ge(S(f"m0_slots{ahead}"), (i + (v + 2) // TURN) * 16 + 16)
                        pool.wait_ge(S("m0_x_turned"), m + 1)
                        settle(pool, S("settled_pool"))
                        gather(ahead, v % 2)
                    for v in (2 * pair, 2 * pair + 1):
                        m = i * TURN + v
                        if v:
                            pool.wait_ge(S("m0_added"), m * 16 * SC)
                        pool.wait_ge(S("m0_y_weighted"), m * SC + SC)
                        settle(pool, S("settled_pool"))
                        for c in range(SC):
                            pool.indirect_dma_start(out=k.acc, out_offset=bass.IndirectOffsetOnAxis(ap=slots[:, v, c, 0:1], axis=0),
                                                    in_=yw[:, v, c, :], in_offset=None, compute_op=ALU.add
                                                    ).then_inc(S("m0_added"), 16)
                pool.wait_ge(S("m0_added"), (i * TURN + TURN) * 16 * SC)
            for u in range(2):
                pool.wait_ge(S(f"m0_x{u}"), (count * 2 + 1) * 16 * SC)
            pool.wait_ge(S("m0_added"), count * (16 * SC * TURN))

        @block.tensor
        def _(pe):
            pe.matmul(bank[B_C][:, 0:E0], k.ones_bf[:], k.count0[:, 0], start=True, stop=True).then_inc(S("m0_counted"), 1)
            pe.wait_ge(S("m0_shared_cast"), 1)

            def shared_hidden(g):
                for n in range(2):
                    if g >= 2:
                        pe.wait_ge(S("m0s_hf"), g - 1)
                    for j, (part, c) in enumerate((a, b) for a in (k.zhi, k.zlo) for b in range(KD)):
                        mm = pe.matmul(bank[2 * (g % 2) + n][:], w13(shared, n, c), part[:, c, g * 512:(g + 1) * 512],
                                       start=j == 0, stop=j == 2 * KD - 1)
                mm.then_inc(S("m0s_h"), 1)

            def shared_out(g):
                pe.wait_ge(S("m0s_hl"), g + 1)
                for c in range(SG):
                    if c % 2 == 0 and g:
                        pe.wait_ge(S("m0s_added"), 2 * g - 1 + c // 2)
                    for part, first in ((hhs, True), (hls, False)):
                        mm = pe.matmul(bank[4 + c // 2][:, c % 2 * D:(c % 2 + 1) * D], part[:, g % 2, c * P:(c + 1) * P],
                                       shared[:, 2 * D:3 * D], start=first, stop=not first)
                    if c % 2:
                        mm.then_inc(S("m0s_y"), 1)
            for g in range(TILES // SG + 1):
                if g < TILES // SG:
                    shared_hidden(g)
                if g:
                    shared_out(g - 1)
            pe.wait_ge(S("m0s_added"), 2 * TILES // SG)
            pe.wait_ge(S("m0_listed"), 2)
            count = pe.value_load(turns[0:1, 0:1], min_val=1, max_val=E0 // TURN)
            with pe.Fori(0, count) as i:
                for pair in range(TURN // 2):
                    both = [(i * TURN + v, v % 2, v) for v in (2 * pair, 2 * pair + 1)]
                    for m, u, v in both:
                        pe.wait_ge(S(f"m0_x{u}"), (i * 2 + v // 2) * 16 * SC + 16 * SC)
                        for d in range(KD):
                            for c in range(SC):
                                mm = pe.transpose(bank[B_X + u][:, d * CAP0 + c * P:d * CAP0 + (c + 1) * P],
                                                  x[:, u, c, d * P:(d + 1) * P], k.ident[:])
                        mm.then_inc(S("m0_x_turned"), 1)
                    for m, u, v in both:
                        pe.wait_ge(S("m0_cast"), m + 1)
                        pe.wait_ge(S("m0_xl"), m + 1)
                        for n in range(2):
                            for j, (part, d) in enumerate((a, b) for a in (xh, xl) for b in range(KD)):
                                mm = pe.matmul(bank[B_H + u][:, n * CAP0:(n + 1) * CAP0], w13(wts[:, u], n, d), part[:, u, d],
                                               start=j == 0, stop=j == 2 * KD - 1)
                        mm.then_inc(S("m0_h"), 1)
                    for m, u, v in both:
                        pe.wait_ge(S("m0_hl"), m + 1)
                        for c in range(SC):
                            for part, first in ((hh, True), (hl, False)):
                                mm = pe.matmul(bank[B_Y + u][:, c * D:(c + 1) * D], part[:, u, c * P:(c + 1) * P],
                                               wts[:, u, 2 * D:3 * D], start=first, stop=not first)
                        mm.then_inc(S("m0_y"), 1)
                    pe.wait_ge(S("m0_y_weighted"), (i * TURN + 2 * pair + 2) * SC)

        @block.scalar
        def _(act):
            act.preload_act_table(ACT.Silu)
            for g in range(TILES // SG):
                act.wait_ge(S("m0s_h"), g + 1)
                if g >= 2:
                    act.wait_ge(S("m0s_hf"), g - 1)
                act.activation(sgs[:, g % 2], bank[2 * (g % 2)][:], ACT.Silu).then_inc(S("m0s_sg"), 1)
            act.wait_ge(S("m0_listed"), 2)
            count = act.value_load(turns[0:1, 0:1], min_val=1, max_val=E0 // TURN)
            with act.Fori(0, count) as i:
                for pair in range(TURN // 2):
                    both = [(i * TURN + v, v % 2, v) for v in (2 * pair, 2 * pair + 1)]
                    for m, u, v in both:
                        act.wait_ge(S("m0_x_turned"), m + 1)
                        act.copy(xh[:, u].rearrange("p d s -> p (d s)"), bank[B_X + u][:]).then_inc(S("m0_xh"), 1)
                    for m, u, v in both:
                        act.wait_ge(S("m0_h"), m + 1)
                        act.activation(sg[:, u], bank[B_H + u][:, 0:CAP0], ACT.Silu).then_inc(S("m0_sg"), 1)
                    for m, u, v in both:
                        act.wait_ge(S("m0_y"), m + 1)
                        act.wait_ge(S(f"m0_slots{v}"), i * 16 + 16)
                        for c in range(SC):
                            act.activation(yw[:, v, c], bank[B_Y + u][:, c * D:(c + 1) * D], ACT.Copy,
                                           scale=slots[:, v, c, 1:2].bitcast(F32)).then_inc(S("m0_y_weighted"), 1)

        @block.vector
        def _(dve):
            def chain(ins, n):
                ins.then_inc(S("m0_list_steps"), 1)
                dve.wait_ge(S("m0_list_steps"), n)
            dve.wait_ge(S("m0_shared_loaded"), 16)
            dve.tensor_copy(shared[:], shared_bf[:]).then_inc(S("m0_shared_cast"), 1)
            dve.memset(order[:], 0).then_inc(S("m0_order_set"), 1)
            dve.memset(tsh[:], 0.0).then_inc(S("m0_order_set"), 1)
            dve.wait_ge(S("m0_order_set"), 2)
            dve.wait_ge(S("m0_counted"), 1)
            chain(dve.tensor_scalar(active[:], bank[B_C][:, 0:E0], 0.0, None, ALU.is_gt), 1)
            chain(dve.tensor_tensor_scan(upto[:], active[:], tsh[:], 0.0, ALU.add, ALU.add), 2)
            chain(dve.tensor_scalar(idle[:], k.iota_e[:], upto[:, E0 - 1:E0], None, ALU.add), 3)
            chain(dve.tensor_tensor(idle[:], idle[:], upto[:], ALU.subtract), 4)
            chain(dve.scalar_tensor_tensor(place[:], upto[:], -1.0, idle[:], ALU.add, ALU.subtract), 5)
            chain(dve.tensor_tensor(place2[:], place[:], active[:], ALU.mult), 6)
            chain(dve.tensor_tensor(place[:], place2[:], idle[:], ALU.add), 7)
            chain(dve.tensor_tensor(is_at[:], bc(k.iota_e[:].unsqueeze(2), [P, E0, E0]), bc(place[:].unsqueeze(1), [P, E0, E0]),
                                    ALU.is_equal), 8)
            chain(dve.tensor_tensor(named[:], is_at[:], bc(k.iota_e[:].unsqueeze(1), [P, E0, E0]), ALU.mult), 9)
            with nc.allow_low_precision("numbers of experts"):
                dve.tensor_reduce(order[:, 0:E0], named[:], AX.X, ALU.add).then_inc(S("m0_listed"), 1)
            chain(dve.tensor_scalar(up3[:], upto[:, E0 - 1:E0], float(TURN - 1), None, ALU.add), 10)
            chain(dve.tensor_copy(up3i[:], up3[:]), 11)
            dve.tensor_scalar(turns[:], up3i[:], TURN.bit_length() - 1, None, ALU.logical_shift_right).then_inc(S("m0_listed"), 1)
            for g in range(TILES // SG + 1):
                if g < TILES // SG:
                    dve.wait_ge(S("m0s_sg"), g + 1)
                    dve.tensor_tensor(hfs[:, g % 2], sgs[:, g % 2], bank[2 * (g % 2) + 1][:], ALU.mult).then_inc(S("m0s_hf"), 1)
                    dve.wait_ge(S("m0s_hf"), g + 1)
                    dve.tensor_copy(hhs[:, g % 2], hfs[:, g % 2]).then_inc(S("m0s_hh"), 1)
                    dve.wait_ge(S("m0s_hh"), g + 1)
                    dve.tensor_tensor(hls[:, g % 2], hfs[:, g % 2], hhs[:, g % 2].bitcast(F32), ALU.subtract
                                      ).then_inc(S("m0s_hl"), 1)
                if g:
                    for c in range(SG // 2):
                        dve.wait_ge(S("m0s_y"), 2 * (g - 1) + c + 1)
                        rows = k.h[:, (g - 1) * SG + 2 * c:(g - 1) * SG + 2 * c + 2, :].rearrange("p t d -> p (t d)")
                        dve.tensor_tensor(rows, rows, bank[4 + c][:], ALU.add).then_inc(S("m0s_added"), 1)
            dve.wait_ge(S("m0_listed"), 2)
            count = dve.value_load(turns[0:1, 0:1], min_val=1, max_val=E0 // TURN)
            for u in range(2):
                dve.wait_ge(S(f"m0_raw{u}"), 16)
                dve.tensor_copy(wts[:, u], raw[:, u]).then_inc(S("m0_cast"), 1)
            with dve.Fori(0, count) as i:
                for pair in range(TURN // 2):
                    both = [(i * TURN + v, v % 2, v) for v in (2 * pair, 2 * pair + 1)]
                    for m, u, v in both:
                        dve.wait_ge(S("m0_xh"), m + 1)
                        dve.tensor_tensor(xl[:, u].rearrange("p d s -> p (d s)"), bank[B_X + u][:],
                                          xh[:, u].rearrange("p d s -> p (d s)").bitcast(F32), ALU.subtract
                                          ).then_inc(S("m0_xl"), 1)
                    for m, u, v in both:
                        dve.wait_ge(S("m0_sg"), m + 1)
                        dve.tensor_tensor(hf[:, u], sg[:, u], bank[B_H + u][:, CAP0:2 * CAP0], ALU.mult).then_inc(S("m0_hf"), 1)
                        dve.wait_ge(S("m0_hf"), m + 1)
                        dve.tensor_copy(hh[:, u], hf[:, u]).then_inc(S("m0_hh"), 1)
                        dve.wait_ge(S("m0_hh"), m + 1)
                        dve.tensor_tensor(hl[:, u], hf[:, u], hh[:, u].bitcast(F32), ALU.subtract).then_inc(S("m0_hl"), 1)
                    for m, u, v in both:
                        dve.wait_ge(S("m0_y"), m + 1)
                        dve.wait_ge(S(f"m0_raw{u}"), (i * 2 + v // 2 + 1) * 16 + 16)
                        dve.tensor_copy(wts[:, u], raw[:, u]).then_inc(S("m0_cast"), 1)


def last_attention(k):
    nc, S = k.nc, k.S
    with ExitStack() as ctx:
        sb = lambda n, s, d: k.sb("la_" + n, s, d, ctx)
        bank = k.bank
        ac = sb("ac", [P, 2, D], F32)
        z, zT = sb("z", [P, 2, D], F32), sb("zT", [P, 2, KD, P], F32)
        qk, v = sb("qk", [P, 2, 2, KD, P], F32), sb("v", [P, 2, D], F32)
        mx, shift = sb("mx", [P, 2], F32), sb("shift", [P, 2], F32)
        probs, total, recip = sb("probs", [P, 2, P], F32), sb("total", [P, 2], F32), sb("recip", [P, 2], F32)
        pT = sb("pT", [P, 2, P], F32)
        z3, z3T = sb("z3", [P, 2, D], F32), sb("z3T", [P, 2, KD, P], F32)
        base = sb("base", [P, 2, D], F32)
        statsa, agga = sb("statsa", [P, 2, 6], F32), sb("agga", [P, 2, 2], F32)
        lmax, centred, ex = sb("lmax", [P, 2, 1], F32), sb("centred", [P, 2, E1], F32), sb("ex", [P, 2, E1], F32)
        esum, erecip, prob = sb("esum", [P, 2, 1], F32), sb("erecip", [P, 2, 1], F32), sb("prob", [P, 2, E1], F32)
        top, topi = sb("top", [P, 2, 8], F32), sb("topi", [P, 2, 8], U32)
        choice, onehot = sb("choice", [P, 2, K1], F32), sb("onehot", [P, 2, K1, E1], F32)
        chosen, both = sb("chosen", [P, 2, E1], BF16), sb("both", [P, E1], BF16)
        ranked, rank = sb("ranked", [P, 2, K1, E1], F32), sb("rank", [P, 2, K1], F32)
        kept, slot, slot2 = sb("kept", [P, 2, K1], F32), sb("slot", [P, 2, K1], F32), sb("slot2", [P, 2, K1], F32)
        wsum, wr = sb("wsum", [P, 2, 1], F32), sb("wr", [P, 2, 1], F32)
        to, pay = sb("to", [P, 2, K1], U32), sb("pay", [P, 2, K1, 2], U32)
        B_ZT, B_QK, B_V, B_S, B_PT, B_O, B_Z3T, B_R = range(8)
        LOGITS, RANKS = slice(0, 2 * E1), slice(2 * E1, 4 * E1)
        DEPTH, FIRST = 5, 8
        scale = D ** -0.5
        block = ctx.enter_context(nc.Block())

        def pair(t):
            return Pair(t.loop, t.const) if t and t.par else None

        @block.sync
        def _(sp):
            def body(at):
                if a := at(0):
                    a.before(sp, S("la_added"), 2)
                    sp.dma_start(ac[:, a.par], k.acc[bass.ts(a.t, P), :]).then_inc(S(f"la_ac{a.par}"), 16)
                if r := at(4):
                    r.made(sp, S("la_z3"))
                    sp.dma_start(k.z1[bass.ts(r.t, P), :], z3[:, r.par]).then_inc(S(f"la_stored{r.par}"), 16)
                    r.made(sp, S("la_base"))
                    sp.dma_start(k.out[bass.ts(r.t, P), :], base[:, r.par]).then_inc(S(f"la_out{r.par}"), 16)
            steps(sp, body, TILES, DEPTH, FIRST)
            for par in range(2):
                sp.wait_ge(S(f"la_stored{par}"), 16 * TILES // 2)
                sp.wait_ge(S(f"la_out{par}"), 16 * TILES // 2)

        @block.tensor
        def _(pe):
            def body(at):
                f, s, p, r, w_ = (at(n) for n in range(1, 6))
                rr, ww = pair(r), pair(w_)
                if s:
                    s.made(pe, S("la_qk"))
                    s.before(pe, S("la_probs"), 1)
                    for c in range(KD):
                        pe.matmul(bank[B_S][:, 0:P], qk[:, s.par, 0, c], qk[:, s.par, 1, c], start=c == 0, stop=False)
                    pe.matmul(bank[B_S][:, 0:P], k.ident_bf[:], k.causal[:], start=False, stop=True
                              ).then_inc(S("la_scores"), 1)
                if p:
                    p.made(pe, S("la_probs"))
                    p.before(pe, S("la_pT"), 1)
                    pe.transpose(bank[B_PT][:, 0:P], probs[:, p.par], k.ident[:]).then_inc(S("la_pT_turned"), 1)
                if f:
                    f.made(pe, S("la_z"))
                    f.before(pe, S("la_zT"), 1)
                    for c in range(KD):
                        mm = pe.transpose(bank[B_ZT][:, c * P:(c + 1) * P], z[:, f.par, c * P:(c + 1) * P], k.ident[:])
                    mm.then_inc(S("la_zT_turned"), 1)
                if r:
                    r.made(pe, S("la_z3"))
                    r.before(pe, S("la_z3T"), 1)
                    for c in range(KD):
                        mm = pe.transpose(bank[B_Z3T][:, c * P:(c + 1) * P], z3[:, r.par, c * P:(c + 1) * P], k.ident[:])
                    mm.then_inc(S("la_z3T_turned"), 1)
                if p:
                    p.made(pe, S("la_pT"))
                    p.made(pe, S("la_v"))
                    p.before(pe, S("la_h"), 1)
                    pe.matmul(bank[B_O][:, 0:D], pT[:, p.par], v[:, p.par], start=True, stop=True).then_inc(S("la_o"), 1)
                if f:
                    f.made(pe, S("la_zT"))
                    f.before(pe, S("la_qk"), 1)
                    for n in range(2):
                        for c in range(2):
                            for d in range(KD):
                                mm = pe.matmul(bank[B_QK][:, (2 * n + c) * P:(2 * n + c + 1) * P],
                                               k.wqkv1[:, n, d, c * P:(c + 1) * P], zT[:, f.par, d],
                                               start=d == 0, stop=d == KD - 1)
                    mm.then_inc(S("la_qk_projected"), 1)
                    f.before(pe, S("la_v"), 1)
                    for d in range(KD):
                        mm = pe.matmul(bank[B_V][:, 0:D], zT[:, f.par, d], k.wqkv1[:, 2, d], start=d == 0, stop=d == KD - 1)
                    mm.then_inc(S("la_v_projected"), 1)
                if r:
                    r.made(pe, S("la_z3T"))
                    Pair(r.loop, r.const).before(pe, S("r1_ranked" if rr else "r1_centred"), 1)
                    for d in range(KD):
                        mm = pe.matmul(bank[B_R][:, r.par * E1:(r.par + 1) * E1], z3T[:, r.par, d], k.router[:, d],
                                       start=d == 0, stop=d == KD - 1)
                    mm.then_inc(S("la_logits"), 1)
                if ww:
                    ww.made(pe, S("r1_chosen"))
                    ww.before(pe, S("r1_counted"), 1)
                    pe.matmul(bank[B_R][:, RANKS], k.before[:], chosen[:].rearrange("p t e -> p (t e)"), start=True, stop=False)
                    pe.matmul(bank[B_R][:, RANKS.start + E1:RANKS.stop], k.ones_bf[:], chosen[:, 0], start=False, stop=False)
                    pe.matmul(bank[B_R][:, RANKS].rearrange("p (t e) -> p t e", t=2), k.ones_bf[:],
                              bc(k.count1[:].unsqueeze(1), [P, 2, E1]), start=False, stop=True).then_inc(S("r1_ranks"), 1)
            steps(pe, body, TILES, DEPTH, FIRST)

        @block.scalar
        def _(act):
            act.preload_act_table(ACT.Exp)

            def body(at):
                f, s, p, r = (at(n) for n in range(1, 5))
                rr = pair(r)
                if f:
                    f.made(act, S("la_zT_turned"))
                    f.before(act, S("la_v_projected"), 2)
                    act.copy(zT[:, f.par].rearrange("p c q -> p (c q)"), bank[B_ZT][:, 0:D]).then_inc(S("la_zT"), 1)
                if r:
                    r.made(act, S("la_z3T_turned"))
                    r.before(act, S("la_logits"), 2)
                    act.copy(z3T[:, r.par].rearrange("p c q -> p (c q)"), bank[B_Z3T][:, 0:D]).then_inc(S("la_z3T"), 1)
                if s:
                    s.made(act, S("la_shift"))
                    s.before(act, S("la_pT_turned"), 2)
                    act.activation(probs[:, s.par], bank[B_S][:, 0:P], ACT.Exp, bias=shift[:, s.par:s.par + 1], scale=scale,
                                   accum_out=total[:, s.par:s.par + 1]).then_inc(S("la_probs"), 1)
                if f:
                    f.made(act, S("la_qk_projected"))
                    f.before(act, S("la_scores"), 2)
                    act.copy(qk[:, f.par].rearrange("p n c q -> p (n c q)"), bank[B_QK][:]).then_inc(S("la_qk"), 1)
                if rr:
                    rr.made(act, S("r1_centred"))
                    rr.before(act, S("r1_prob"), 1)
                    act.activation(ex[:], centred[:], ACT.Exp).then_inc(S("r1_ex"), 1)
            steps(act, body, TILES, DEPTH, FIRST)

        @block.vector
        def _(dve):
            dve.memset(k.count1[:], 0.0).then_inc(S("la_set"), 1)
            dve.wait_ge(S("la_set"), 1)

            def norm(t, tag, stats, agg):
                t.made(dve, S(f"la_{tag}"))
                settle(dve, S("settled_dve"))
                dve.bn_stats(stats[:, t.par], k.h[:, t.t, :]).then_inc(S(f"la_{tag}_stats"), 1)
                yield
                t.made(dve, S(f"la_{tag}_stats"))
                settle(dve, S("settled_dve"))
                dve.bn_aggr(agg[:, t.par], stats[:, t.par]).then_inc(S(f"la_{tag}_mv"), 1)
                yield
                t.made(dve, S(f"la_{tag}_mv"))
                dve.tensor_tensor(k.mv[:, t.t, :], agg[:, t.par], k.eps[:], ALU.add
                                  ).then_inc(S(f"la_{tag}_ve"), 1)
                yield

            def route(rr):
                logits = bank[B_R][:, LOGITS].rearrange("p (t e) -> p t e", t=2)
                rr.made(dve, S("la_logits"), 2)
                dve.tensor_reduce(lmax[:], logits, AX.X, ALU.max).then_inc(S("r1_max"), 1)
                rr.made(dve, S("r1_max"))
                rr.before(dve, S("r1_ex"), 1)
                dve.tensor_tensor(centred[:], logits, bc(lmax[:], [P, 2, E1]), ALU.subtract).then_inc(S("r1_centred"), 1)
                rr.made(dve, S("r1_ex"))
                dve.tensor_reduce(esum[:], ex[:], AX.X, ALU.add).then_inc(S("r1_esum"), 1)
                rr.made(dve, S("r1_esum"))
                dve.reciprocal(erecip[:], esum[:]).then_inc(S("r1_erecip"), 1)
                rr.made(dve, S("r1_erecip"))
                dve.tensor_tensor(prob[:], ex[:], bc(erecip[:], [P, 2, E1]), ALU.mult).then_inc(S("r1_prob"), 1)
                rr.made(dve, S("r1_prob"))
                for t in range(2):
                    settle(dve, S("settled_dve"))
                    dve.max(top[:, t], prob[:, t]).then_inc(S("r1_top"), 1)
                for t in range(2):
                    rr.made(dve, S("r1_top"), 2, t + 1)
                    settle(dve, S("settled_dve"))
                    dve.max_index(topi[:, t], top[:, t], prob[:, t]).then_inc(S("r1_topi"), 1)
                rr.made(dve, S("r1_topi"), 2)
                dve.tensor_copy(choice[:], topi[:, :, 0:K1]).then_inc(S("r1_choice"), 1)
                rr.made(dve, S("r1_choice"))
                dve.tensor_tensor(onehot[:], bc(k.iota_e[:, 0:E1].unsqueeze(1).unsqueeze(1), [P, 2, K1, E1]),
                                  bc(choice[:].unsqueeze(3), [P, 2, K1, E1]), ALU.is_equal).then_inc(S("r1_onehot"), 1)
                rr.made(dve, S("r1_onehot"))
                with nc.allow_low_precision("counts of 0 and 1"):
                    dve.tensor_reduce(chosen[:], onehot[:].rearrange("p t n e -> p t e n"), AX.X, ALU.add
                                      ).then_inc(S("r1_chosen"), 1)
                rr.made(dve, S("r1_chosen"))
                dve.tensor_tensor(both[:], chosen[:, 0], chosen[:, 1], ALU.add).then_inc(S("r1_both"), 1)

            def weights(ww):
                ww.made(dve, S("r1_ranks"))
                dve.tensor_tensor(ranked[:], onehot[:],
                                  bc(bank[B_R][:, RANKS].rearrange("p (t e) -> p t e", t=2).unsqueeze(2), [P, 2, K1, E1]),
                                  ALU.mult).then_inc(S("r1_ranked"), 1)
                yield
                ww.made(dve, S("r1_both"))
                dve.tensor_tensor(k.count1[:], k.count1[:], both[:], ALU.add).then_inc(S("r1_counted"), 1)
                dve.tensor_reduce(wsum[:], top[:, :, 0:K1], AX.X, ALU.add).then_inc(S("r1_wsum"), 1)
                yield
                ww.made(dve, S("r1_ranked"))
                dve.tensor_reduce(rank[:], ranked[:], AX.X, ALU.add).then_inc(S("r1_rank"), 1)
                yield
                ww.made(dve, S("r1_wsum"))
                dve.reciprocal(wr[:], wsum[:]).then_inc(S("r1_wr"), 1)
                yield
                ww.made(dve, S("r1_rank"))
                dve.tensor_scalar(kept[:], rank[:], float(CAP1), None, ALU.is_lt).then_inc(S("r1_kept"), 1)
                dve.scalar_tensor_tensor(slot[:], choice[:], float(STRIDE1), rank[:], ALU.mult, ALU.add
                                         ).then_inc(S("r1_slot"), 1)
                if ww.const:
                    dve.wait_ge(S("r1_scattered"), ww.t * 32 * K1)
                dve.tensor_copy(pay[:, :, :, 0], bc(k.ids[:, bass.ds(ww.t * 2, 2)].unsqueeze(2), [P, 2, K1])
                                ).then_inc(S("r1_pay"), 1)
                yield
                ww.made(dve, S("r1_kept"))
                ww.made(dve, S("r1_slot"))
                dve.scalar_tensor_tensor(slot2[:], slot[:], k.trash1[:, 0:1], kept[:], ALU.subtract, ALU.mult
                                         ).then_inc(S("r1_slot2"), 1)
                ww.made(dve, S("r1_wr"))
                dve.tensor_tensor(pay[:, :, :, 1].bitcast(F32), top[:, :, 0:K1], bc(wr[:], [P, 2, K1]), ALU.mult
                                  ).then_inc(S("r1_pay"), 1)
                yield
                ww.made(dve, S("r1_slot2"))
                dve.tensor_scalar(to[:], slot2[:], k.trash1[:, 0:1], None, ALU.add).then_inc(S("r1_to"), 1)

            def body(at):
                a, f, s, p, r, w_ = (at(n) for n in range(6))
                rr, ww = pair(r), pair(w_)
                small = weights(ww) if ww else iter(())
                norm_a = iter(())
                if f:
                    f.made(dve, S("la_a_rstd"))
                    f.before(dve, S("la_zT_turned"), 2)
                    dve.tensor_scalar(z[:, f.par], k.h[:, f.t, :], k.mv[:, f.t, 0:1], k.rstd[:, bass.ds(f.t, 1)],
                                      ALU.subtract, ALU.mult).then_inc(S("la_z"), 1)
                if s:
                    s.made(dve, S("la_scores"))
                    s.before(dve, S("la_shift"), 2)
                    dve.tensor_reduce(mx[:, s.par:s.par + 1], bank[B_S][:, 0:P], AX.X, ALU.max).then_inc(S("la_max"), 1)
                if p:
                    p.made(dve, S("la_pT_turned"))
                    p.before(dve, S("la_o"), 2)
                    dve.tensor_copy(pT[:, p.par], bank[B_PT][:, 0:P]).then_inc(S("la_pT"), 1)
                if s:
                    s.made(dve, S("la_max"))
                    s.before(dve, S("la_probs"), 2)
                    dve.tensor_scalar(shift[:, s.par:s.par + 1], mx[:, s.par:s.par + 1], -scale, None, ALU.mult
                                      ).then_inc(S("la_shift"), 1)
                if r:
                    r.made(dve, S("la_h_rstd"))
                    r.before(dve, S("la_base"), 2)
                    if r.const >= 2:
                        dve.wait_ge(S(f"la_stored{r.par}"), r.lap() * 16)
                    dve.tensor_scalar(z3[:, r.par], k.h[:, r.t, :], k.mv[:, r.t, 0:1], k.rstd[:, bass.ds(r.t, 1)],
                                      ALU.subtract, ALU.mult).then_inc(S("la_z3"), 1)
                next(small, None)
                if a:
                    dve.wait_ge(S(f"la_ac{a.par}"), a.lap() * 16 + 16)
                    dve.tensor_tensor(k.h[:, a.t, :], k.h[:, a.t, :], ac[:, a.par], ALU.add).then_inc(S("la_added"), 1)
                    norm_a = norm(a, "added", statsa, agga)
                if p:
                    dve.reciprocal(recip[:, p.par:p.par + 1], total[:, p.par:p.par + 1]).then_inc(S("la_recip"), 1)
                next(small, None)
                next(norm_a, None)
                if p:
                    p.made(dve, S("la_recip"))
                    p.made(dve, S("la_o"))
                    dve.scalar_tensor_tensor(k.h[:, p.t, :], bank[B_O][:, 0:D], recip[:, p.par:p.par + 1], k.h[:, p.t, :],
                                             ALU.mult, ALU.add).then_inc(S("la_h"), 1)
                    norm_p = norm(p, "h", k.stats, k.agg)
                else:
                    norm_p = iter(())
                for _ in range(2):
                    next(norm_a, None)
                    next(norm_p, None)
                    next(small, None)
                for _ in norm_a:
                    pass
                if f:
                    f.made(dve, S("la_v_projected"))
                    f.before(dve, S("la_o"), 2)
                    dve.tensor_copy(v[:, f.par], bank[B_V][:, 0:D]).then_inc(S("la_v"), 1)
                for _ in norm_p:
                    pass
                for _ in small:
                    pass
                if rr:
                    route(rr)
            steps(dve, body, TILES, DEPTH, FIRST)

        @block.gpsimd
        def _(pool):
            def body(at):
                a, p, r, ww = at(0), at(3), at(4), pair(at(5))
                if r:
                    r.made(pool, S("la_z3"))
                    if r.const >= 2:
                        pool.wait_ge(S(f"la_out{r.par}"), r.lap() * 16)
                    pool.tensor_tensor(base[:, r.par], k.h[:, r.t, :], z3[:, r.par], ALU.add).then_inc(S("la_base"), 1)
                for t, tag, made in ((a, "added", "a"), (p, "h", "h")):
                    if t:
                        t.made(pool, S(f"la_{tag}_ve"))
                        pool.tensor_tensor(k.rstd[:, bass.ds(t.t, 1)], k.mv[:, t.t, 1:2], k.nhalf[:], ALU.pow
                                           ).then_inc(S(f"la_{made}_rstd"), 1)
                if ww:
                    ww.made(pool, S("r1_to"))
                    ww.made(pool, S("r1_pay"), 2)
                    settle(pool, S("settled_pool"))
                    for t in range(2):
                        for n in range(K1):
                            pool.indirect_dma_start(out=k.table1, out_offset=bass.IndirectOffsetOnAxis(ap=to[:, t, n:n + 1], axis=0),
                                                    in_=pay[:, t, n, :], in_offset=None, bounds_check=E1 * STRIDE1 - 1,
                                                    oob_is_err=False).then_inc(S("r1_scattered"), 16)
            steps(pool, body, TILES, DEPTH, FIRST)
            pool.wait_ge(S("r1_scattered"), 16 * K1 * TILES)


def second_mixture(k):
    nc, S = k.nc, k.S
    SC = -(-SLOTS1 // P)
    LAST = SLOTS1 - (SC - 1) * P
    HALF = SLOTS1 // 2
    ROUNDS = SC // 2
    ALL = 16 * SC
    with ExitStack() as ctx:
        sb = lambda n, s, d: k.sb("m1_" + n, s, d, ctx)
        bank = k.bank
        slots = sb("slots", [P, 2, SC, 2], U32)
        x = sb("x", [P, 2, SC, D], F32)
        raw = [sb(f"raw{n}", [P, FC1 * D], F32) for n in (1, 2)]
        hi = [sb(f"w{n}h", [P, FC1 * D], F32R) for n in (1, 2)]
        lo = [sb(f"w{n}l", [P, FC1 * D], F32R) for n in (1, 2)]
        xh, xl = sb("xh", [P, KD, SLOTS1], F32R), sb("xl", [P, KD, SLOTS1], F32R)
        hf = sb("hf", [P, 2, SLOTS1], F32)
        hh, hl = sb("hh", [P, FC1, SLOTS1], F32R), sb("hl", [P, FC1, SLOTS1], F32R)
        yw = sb("yw", [P, SC, D], F32)
        B_H, B_Y, B_X = 0, 4, 6
        table_rows = k.table1[0:E1 * STRIDE1, :].rearrange("(e c p) w -> e p c w", e=E1, p=P)
        w1 = [t[:].rearrange("p (d f) -> p d f", d=KD) for t in (hi[0], lo[0])]
        w2 = [t[:].rearrange("p (f d) -> p f d", f=FC1) for t in (hi[1], lo[1])]
        DEPTH, FIRST = 1, 2
        block = ctx.enter_context(nc.Block())

        def rows(c):
            return P if c < SC - 1 else LAST

        def turned(r, tile, b):
            n = rows(2 * r) + rows(2 * r + 1)
            return tile[:, :, 2 * r * P:2 * r * P + n], bank[B_X + b][:].rearrange("p (d s) -> p d s", d=KD)[:, :, 0:n]

        @block.sync
        def _(sp):
            def body(at):
                if x_ := at(0):
                    x_.before(sp, S("m1_w1_lo"), 1)
                    sp.dma_start(raw[0][:], k.io["w1"][x_.t]).then_inc(S("m1_raw1"), 16)
                    if x_.const >= 2:
                        sp.wait_ge(S("m1_added"), (x_.t - 1) * ALL)
                    sp.dma_start(slots[:, x_.par], table_rows[x_.t]).then_inc(S(f"m1_slots{x_.par}"), 16)
                    x_.before(sp, S("m1_w2_lo"), 1)
                    sp.dma_start(raw[1][:], k.io["w2"][x_.t]).then_inc(S("m1_raw2"), 16)
            steps(sp, body, E1, DEPTH, FIRST)

        @block.gpsimd
        def _(pool):
            def body(at):
                x_, c_ = at(0), at(1)
                if x_:
                    pool.wait_ge(S(f"m1_slots{x_.par}"), x_.lap() * 16 + 16)
                    x_.before(pool, S("m1_x_turned"), 2, ROUNDS)
                    settle(pool, S("settled_pool"))
                    for c in range(SC):
                        n = rows(c)
                        pool.indirect_dma_start(out=x[0:n, x_.par, c, :], out_offset=None, in_=k.z1,
                                                in_offset=bass.IndirectOffsetOnAxis(ap=slots[0:n, x_.par, c, 0:1], axis=0)
                                                ).then_inc(S(f"m1_x{x_.par}"), 16)
                if c_:
                    for c in range(SC):
                        n = rows(c)
                        c_.made(pool, S("m1_y_weighted"), SC, c + 1)
                        if c == 0:
                            c_.before(pool, S("m1_added"), 1, ALL)
                        settle(pool, S("settled_pool"))
                        pool.indirect_dma_start(out=k.out, out_offset=bass.IndirectOffsetOnAxis(ap=slots[0:n, c_.par, c, 0:1], axis=0),
                                                in_=yw[0:n, c, :], in_offset=None, compute_op=ALU.add
                                                ).then_inc(S("m1_added"), 16)
            steps(pool, body, E1, DEPTH, FIRST)
            pool.wait_ge(S("m1_added"), E1 * ALL)

        @block.tensor
        def _(pe):
            def hidden(c_):
                c_.made(pe, S("m1_w1_lo"))
                c_.made(pe, S("m1_xl"), ROUNDS)
                for f in range(FC1):
                    if f >= 2:
                        c_.made(pe, S("m1_hf"), FC1, f - 1)
                    else:
                        c_.before(pe, S("m1_hf"), 1, FC1, f + FC1 - 1)
                    passes = [(w1[0], xh), (w1[0], xl), (w1[1], xh)]
                    for j, (w, part) in enumerate(passes):
                        for d in range(KD):
                            for s in range(2):
                                mm = pe.matmul(bank[B_H + 2 * (f % 2) + s][:, 0:HALF], w[:, d, f * P:(f + 1) * P],
                                               part[:, d, s * HALF:(s + 1) * HALF],
                                               start=j == 0 and d == 0, stop=j == len(passes) - 1 and d == KD - 1)
                    mm.then_inc(S("m1_h"), 1)

            def output(c_, c):
                n = rows(c)
                if c == 0:
                    c_.made(pe, S("m1_w2_lo"))
                if c >= 2:
                    c_.made(pe, S("m1_y_weighted"), SC, c - 1)
                else:
                    c_.before(pe, S("m1_y_weighted"), 1, SC, c + SC - 1)
                for f in range(FC1):
                    if c == 0:
                        c_.made(pe, S("m1_hl"), FC1, f + 1)
                    for j, (part, w) in enumerate([(hh, w2[0]), (hh, w2[1]), (hl, w2[0])]):
                        mm = pe.matmul(bank[B_Y + c % 2][0:n, 0:D], part[:, f, c * P:c * P + n], w[:, f],
                                       start=f == 0 and j == 0, stop=f == FC1 - 1 and j == 2)
                mm.then_inc(S("m1_y"), 1)

            def turn(x_, r):
                if r == 0:
                    pe.wait_ge(S(f"m1_x{x_.par}"), (x_.lap() + 1) * ALL)
                if r >= 2:
                    x_.made(pe, S("m1_xl"), ROUNDS, r - 1)
                else:
                    x_.before(pe, S("m1_xl"), 1, ROUNDS)
                for d in range(KD):
                    for c in (2 * r, 2 * r + 1):
                        n = rows(c)
                        at_ = d * 2 * P + (c % 2) * P
                        mm = pe.transpose(bank[B_X + r % 2][:, at_:at_ + n], x[0:n, x_.par, c, d * P:(d + 1) * P],
                                          k.ident[0:n, 0:n])
                mm.then_inc(S("m1_x_turned"), 1)

            def body(at):
                x_, c_ = at(0), at(1)
                if c_:
                    hidden(c_)
                for c in range(SC):
                    if c_:
                        output(c_, c)
                    if x_ and c < ROUNDS:
                        turn(x_, c)
            steps(pe, body, E1, DEPTH, FIRST)

        @block.scalar
        def _(act):
            act.preload_act_table(ACT.Silu)

            def upper(e, n):
                e.made(act, S(f"m1_raw{n}"), 16)
                e.before(act, S("m1_h" if n == 1 else "m1_y"), 1, FC1 if n == 1 else SC)
                act.copy(hi[n - 1][:], raw[n - 1][:]).then_inc(S(f"m1_w{n}_hi"), 1)

            def body(at):
                x_, c_ = at(0), at(1)
                if c_:
                    for f in range(FC1):
                        if f >= 2:
                            c_.made(act, S("m1_hl"), FC1, f - 1)
                        else:
                            c_.before(act, S("m1_hl"), 1, FC1, f + FC1 - 1)
                        c_.made(act, S("m1_h"), FC1, f + 1)
                        act.activation(hf[:, f % 2].rearrange("p (s n) -> p s n", s=2),
                                       k.psum[:, B_H + 2 * (f % 2):B_H + 2 * (f % 2) + 2, 0:HALF], ACT.Silu
                                       ).then_inc(S("m1_hf"), 1)
                        if f == 0:
                            c_.before(act, S("m1_y"), 1, SC)
                        c_.made(act, S("m1_hf"), FC1, f + 1)
                        act.copy(hh[:, f], hf[:, f % 2]).then_inc(S("m1_hh"), 1)
                        if f == 1:
                            upper(c_, 2)
                if x_:
                    upper(x_, 1)
                    for r in range(ROUNDS):
                        x_.made(act, S("m1_x_turned"), ROUNDS, r + 1)
                        x_.before(act, S("m1_h"), 1, FC1)
                        to, held = turned(r, xh, r % 2)
                        act.copy(to, held).then_inc(S("m1_xh"), 1)
            steps(act, body, E1, DEPTH, FIRST)

        @block.vector
        def _(dve):
            def lower(e, n):
                e.made(dve, S(f"m1_w{n}_hi"))
                dve.tensor_tensor(lo[n - 1][:], raw[n - 1][:], hi[n - 1][:].bitcast(F32), ALU.subtract
                                  ).then_inc(S(f"m1_w{n}_lo"), 1)

            def weigh(c_, c):
                n = rows(c)
                c_.made(dve, S("m1_y"), SC, c + 1)
                if c == 0:
                    dve.wait_ge(S(f"m1_slots{c_.par}"), c_.lap() * 16 + 16)
                    c_.before(dve, S("m1_added"), 1, ALL)
                dve.tensor_scalar(yw[0:n, c], bank[B_Y + c % 2][0:n, 0:D], slots[0:n, c_.par, c, 1:2].bitcast(F32), None,
                                  ALU.mult).then_inc(S("m1_y_weighted"), 1)

            def body(at):
                x_, c_ = at(0), at(1)
                if c_:
                    for f in range(FC1):
                        c_.made(dve, S("m1_hh"), FC1, f + 1)
                        dve.tensor_tensor(hl[:, f], hf[:, f % 2], hh[:, f].bitcast(F32), ALU.subtract
                                          ).then_inc(S("m1_hl"), 1)
                        if f == 1:
                            lower(c_, 2)
                for c in range(SC):
                    if c == 0 and x_:
                        lower(x_, 1)
                    if c_:
                        weigh(c_, c)
                    if x_ and c < ROUNDS:
                        x_.made(dve, S("m1_xh"), ROUNDS, c + 1)
                        (to, held), (part, _) = turned(c, xl, c % 2), turned(c, xh, c % 2)
                        dve.tensor_tensor(to, held, part.bitcast(F32), ALU.subtract).then_inc(S("m1_xl"), 1)
            steps(dve, body, E1, DEPTH, FIRST)


PHASES = [setup, token_attention, head_attention, first_mixture, last_attention, second_mixture]


def build(nc, io, out, phases=None):
    with ExitStack() as ctx:
        k = Kernel(nc, ctx, io, out)
        allocate(k)
        for phase in phases or PHASES:
            phase(k)
            if phase is first_mixture:
                k.S.clear()
                k.first_ctx.close()


def host_layout(v):
    import numpy as np
    a = {n: np.asarray(x) for n, x in v.items()}

    def rows(w):
        return w.reshape(KD, P, -1).transpose(1, 0, 2)

    heads = [a[f"L0_attn_W{n}"].reshape(D, D).T for n in "qkv"]
    out = {
        "x": a["x"],
        "wqkv": np.stack([rows(w) for w in heads], 1),
        "bqk": np.stack([a[f"L0_attn_b{n}"].reshape(2, P).T for n in "qk"], 1),
        "bv": a["L0_attn_bv"].reshape(D),
        "gate": rows(a["L0_ffn_gate_w"].T),
        "bias": a["L0_ffn_bias"],
        "router": rows(a["L1_ffn_router_w"].T),
        "moe0": np.concatenate([a["L0_ffn_W1"].reshape(E0, KD, P, I0).transpose(0, 2, 1, 3).reshape(E0, P, -1),
                                a["L0_ffn_W3"].reshape(E0, KD, P, I0).transpose(0, 2, 1, 3).reshape(E0, P, -1),
                                a["L0_ffn_W2"]], 2),
        "shared": np.concatenate([rows(a["L0_ffn_sw1"].T).reshape(P, -1), rows(a["L0_ffn_sw3"].T).reshape(P, -1),
                                  a["L0_ffn_sw2"].T], 1),
        "wqkv1": np.stack([rows(a[f"L1_attn_{n}w"]) for n in "QKV"], 1),
        "w1": a["L1_ffn_w1"].reshape(E1, KD, P, I1).transpose(0, 2, 1, 3).reshape(E1, P, -1),
        "w2": a["L1_ffn_w2"].reshape(E1, FC1, P, D).transpose(0, 2, 1, 3).reshape(E1, P, -1),
    }
    return {n: np.ascontiguousarray(x) for n, x in out.items()}


def kernel(**inputs):
    import concourse.bacc as bacc
    from concourse.bass_utils import run_bass_kernel_spmd

    nc = bacc.Bacc("TRN2", target_bir_lowering=False, num_devices=1)
    arrays = host_layout(inputs)
    io = {n: nc.dram_tensor(f"in_{n}", x.shape, mybir.dt.from_np(x.dtype), kind="ExternalInput").ap()
          for n, x in arrays.items()}
    out = nc.dram_tensor("out", (TOKENS + PAD, D), F32, kind="ExternalOutput").ap()
    build(nc, io, out)
    r = run_bass_kernel_spmd(nc, [{f"in_{n}": x for n, x in arrays.items()}], core_ids=[0])
    return r.results[0]["out"][:TOKENS].reshape(TILES, P, D)
```

```python
from contextlib import ExitStack

import concourse.bass as bass
from concourse import mybir

ALU = mybir.AluOpType
ACT = mybir.ActivationFunctionType
AX = mybir.AxisListType
F32 = mybir.dt.float32
F32R = mybir.dt.float32r
BF16 = mybir.dt.bfloat16
U32 = mybir.dt.uint32
I32 = mybir.dt.int32

P = 128
TILES = 16
D = 256
KD = D // P
TOKENS = TILES * P
HEADS, HEAD = 16, 16
GROUPS = 4
E0, K0, CAP0, I0 = 32, 4, 256, 128
E1, K1, CAP1, I1 = 8, 2, 641, 1024
STRIDE1 = 768
SLOTS1 = 656
FC1 = I1 // P
EPS = 1e-5
MASKED = -3e38
PAD0, PAD = 256, 1024


class Sems:

    def __init__(self, nc):
        self.nc, self.made, self.half = nc, {}, ""

    def __call__(self, name):
        if name not in self.made:
            self.made[name] = self.nc.alloc_semaphore(name + self.half)
        return self.made[name]

    def clear(self):
        self.nc.clear_and_free_semaphores(list(self.made.values()))
        self.nc.all_engine_barrier()
        self.made, self.half = {}, "_2"


class Tile:

    def __init__(self, loop, const):
        self.loop, self.const = loop, const
        self.t = const if loop is None else loop * 2 + const
        self.par = const % 2

    def lap(self):
        return self.const // 2 if self.loop is None else self.loop + self.const // 2

    def made(self, eng, sem, per=1, n=None):
        eng.wait_ge(sem, self.t * per + (per if n is None else n))

    def before(self, eng, sem, back, per=1, n=None):
        if self.const >= back:
            eng.wait_ge(sem, (self.t - back) * per + (per if n is None else n))
        else:
            assert self.loop is None


class Pair(Tile):

    def __init__(self, loop, const):
        self.loop, self.const = loop, const // 2
        self.t = const // 2 if loop is None else loop + const // 2


def steps(eng, body, tiles, depth, first):
    assert first >= depth and (tiles - first) % 2 == 0

    def at(loop, const):
        def tile_at(lag):
            c = const - lag
            if loop is None and not 0 <= c < tiles:
                return None
            return Tile(loop, c)
        return tile_at

    for j in range(first):
        body(at(None, j))
    with eng.Fori(0, (tiles - first) // 2) as i:
        for u in range(2):
            body(at(i, first + u))
    for j in range(tiles, tiles + depth):
        body(at(None, j))


def settle(eng, sem):
    eng.sem_inc(sem, 1)


def bc(ap, shape):
    return ap.to_broadcast(shape)


class Kernel:
    def __init__(self, nc, ctx, io, out):
        self.nc, self.ctx, self.io, self.out = nc, ctx, io, out
        self.S = Sems(nc)

    def sb(self, name, shape, dt, ctx=None):
        return (ctx or self.ctx).enter_context(self.nc.sbuf_tensor(name, shape, dt))



def allocate(k):
    nc, sb = k.nc, k.sb
    k.psum = k.ctx.enter_context(nc.psum_tensor("psum", [P, 8, 512], F32))
    k.bank = [k.psum[:, i] for i in range(8)]
    k.h = sb("residual", [P, TILES, D], F32)
    k.ident = sb("ident", [P, P], F32)
    k.ident_bf = sb("ident_bf", [P, P], BF16)
    k.causal = sb("causal", [P, P], BF16)
    k.before = sb("before", [P, P], BF16)
    k.ones_bf = sb("ones_bf", [P, P], BF16)
    k.zeros = sb("zeros", [P, D], F32)
    k.nhalf = sb("nhalf", [P, 1], F32)
    k.parity = sb("parity", [P, 2], F32)
    k.parity_i = sb("parity_i", [P, 2], I32)
    k.iota_e = sb("iota_e", [P, E0], F32)
    k.pidx = sb("pidx", [P, 1], F32)
    k.trash0 = sb("trash0", [P, 1], F32)
    k.trash1 = sb("trash1", [P, 1], F32)
    k.ids = sb("ids", [P, TILES], U32)
    k.stats = sb("stats", [P, 2, 6], F32)
    k.agg = sb("agg", [P, 2, 2], F32)
    k.eps = sb("eps", [P, 2], F32)
    k.mv = sb("mv", [P, TILES, 2], F32)
    k.rstd = sb("rstd", [P, TILES], F32)
    k.wqkv = sb("wqkv", [P, 3, KD, D], F32)
    k.wqkv1 = sb("wqkv1", [P, 3, KD, D], F32)
    k.bqk = sb("bqk", [P, 2, 2], F32)
    k.bv = sb("bv", [P, D], F32)
    k.gate = sb("gate", [P, KD, E0], F32)
    k.gate_bf = sb("gate_bf", [P, KD, E0], BF16)
    k.bias = sb("bias", [P, E0], F32)
    k.shared_bf, k.shared = sb("shared_bf", [P, 3 * D], BF16), sb("shared", [P, 3 * D], F32R)
    k.router = sb("router", [P, KD, E1], F32)
    k.count0 = sb("count0", [P, 2, E0], BF16)
    k.count1 = sb("count1", [P, E1], BF16)
    k.first_ctx = ExitStack()
    k.zhi, k.zlo = (sb(n, [P, KD, TOKENS], F32R, k.first_ctx) for n in ("zhi", "zlo"))
    k.table0 = nc.dram_tensor("table0", (E0 * CAP0 + P, 2), U32).ap()
    k.table1 = nc.dram_tensor("table1", (E1 * STRIDE1 + P, 2), U32).ap()
    k.z0 = nc.dram_tensor("z0", (TOKENS + PAD0, D), F32).ap()
    k.z1 = nc.dram_tensor("z1", (TOKENS + PAD, D), F32).ap()
    k.acc = nc.dram_tensor("acc", (TOKENS + PAD0, D), F32).ap()


def setup(k):
    nc, S, io = k.nc, k.S, k.io
    n0, n1 = (E0 * CAP0 + P) // P, (E1 * STRIDE1 + P) // P
    with ExitStack() as ctx:
        rows0 = k.sb("rows0", [P, n0], I32, ctx)
        rows1 = k.sb("rows1", [P, n1], I32, ctx)
        low0 = k.sb("low0", [P, n0], I32, ctx)
        low1 = k.sb("low1", [P, n1], I32, ctx)
        init0 = k.sb("init0", [P, n0, 2], U32, ctx)
        init1 = k.sb("init1", [P, n1, 2], U32, ctx)
        rowi = k.sb("rowi", [P, 2], I32, ctx)
        block = ctx.enter_context(nc.Block())

        @block.sync
        def _(sp):
            sp.wait_ge(S("init_made"), 4)
            sp.dma_start(k.table0.rearrange("(p c) w -> p (c w)", p=P),
                         init0[:].rearrange("p c w -> p (c w)")).then_inc(S("tables_set"), 16)
            sp.dma_start(k.table1.rearrange("(p c) w -> p (c w)", p=P),
                         init1[:].rearrange("p c w -> p (c w)")).then_inc(S("tables_set"), 16)
        @block.gpsimd
        def _(pool):
            pool.memset(k.ident[:], 0.0).then_inc(S("filled"), 1)
            pool.memset(k.causal[:], 0.0).then_inc(S("filled"), 1)
            pool.memset(k.ones_bf[:], 1.0).then_inc(S("filled"), 1)
            pool.memset(k.zeros[:], 0.0)
            pool.memset(k.nhalf[:], -0.5)
            pool.memset(k.eps[:, 0:1], 0.0)
            pool.memset(k.eps[:, 1:2], EPS)
            pool.wait_ge(S("filled"), 3)
            pool.affine_select(out=k.ident[:], in_=k.ident[:], compare_op=ALU.not_equal, fill=1.0, base=0,
                               pattern=[[-1, P]], channel_multiplier=1).then_inc(S("ident_made"), 1)
            pool.affine_select(out=k.causal[:], in_=k.causal[:], compare_op=ALU.is_ge, fill=MASKED, base=0,
                               pattern=[[-1, P]], channel_multiplier=1)
            pool.affine_select(out=k.before[:], in_=k.ones_bf[:], compare_op=ALU.is_gt, fill=0.0, base=0,
                               pattern=[[1, P]], channel_multiplier=-1)
            pool.iota(k.ids[:], pattern=[[P, TILES]], base=0, channel_multiplier=1)
            pool.iota(rowi[:], pattern=[[0, 2]], base=0, channel_multiplier=1).then_inc(S("iotas"), 1)
            pool.iota(rows0[:], pattern=[[1, n0]], base=0, channel_multiplier=n0).then_inc(S("iotas"), 1)
            pool.iota(rows1[:], pattern=[[1, n1]], base=0, channel_multiplier=n1).then_inc(S("iotas"), 1)
            for out, base, step, mult in ((k.iota_e, 0, 1, 0), (k.pidx, 0, 0, 1), (k.trash0, E0 * CAP0, 0, 1),
                                          (k.trash1, E1 * STRIDE1, 0, 1)):
                pool.iota(out[:], pattern=[[step, out.shape[1]]], base=base, channel_multiplier=mult,
                          allow_small_or_imprecise_dtypes=True)

        @block.vector
        def _(dve):
            dve.wait_ge(S("iotas"), 3)
            dve.memset(init0[:].bitcast(F32), 0.0).then_inc(S("init_zero"), 1)
            dve.memset(init1[:].bitcast(F32), 0.0).then_inc(S("init_zero"), 1)
            dve.tensor_scalar(low0[:], rows0[:], PAD0 - 1, None, ALU.bitwise_and).then_inc(S("low_made"), 1)
            dve.tensor_scalar(low1[:], rows1[:], PAD - 1, None, ALU.bitwise_and).then_inc(S("low_made"), 1)
            dve.tensor_scalar(k.parity_i[:], rowi[:], 4, 1, ALU.logical_shift_right,
                              ALU.bitwise_and).then_inc(S("low_made"), 1)
            dve.wait_ge(S("init_zero"), 2)
            dve.wait_ge(S("low_made"), 3)
            dve.tensor_scalar(init0[:, :, 0], low0[:], float(TOKENS), None, ALU.add).then_inc(S("init_made"), 1)
            dve.tensor_scalar(init1[:, :, 0], low1[:], float(TOKENS), None, ALU.add).then_inc(S("init_made"), 1)
            dve.tensor_scalar(k.parity[:, 0:1], k.parity_i[:, 0:1], -1.0, 1.0, ALU.mult, ALU.add).then_inc(S("init_made"), 1)
            dve.tensor_copy(k.parity[:, 1:2], k.parity_i[:, 1:2]).then_inc(S("init_made"), 1)
            dve.wait_ge(S("ident_made"), 1)
            dve.tensor_copy(k.ident_bf[:], k.ident[:])


def token_attention(k):
    nc, S = k.nc, k.S
    with ExitStack() as ctx:
        sb = lambda n, s, d: k.sb("ta_" + n, s, d, ctx)
        bank = k.bank
        xin, xT = sb("xin", [P, 2, D], F32), sb("xT", [P, 2, KD, P], F32)
        mx, shift = sb("mx", [P, 2], F32), sb("shift", [P, 2], F32)
        probs, total, recip = sb("probs", [P, 2, P], F32), sb("total", [P, 2], F32), sb("recip", [P, 2], F32)
        pT = sb("pT", [P, 2, P], F32)
        scale = D ** -0.5
        block = ctx.enter_context(nc.Block())
        DEPTH, FIRST = 3, 6

        @block.sync
        def _(sp):
            def body(at):
                if t := at(0):
                    t.before(sp, S("ta_xT_turned"), 2)
                    sp.dma_start(xin[:, t.par], k.io["x"][t.t, ::2, :]).then_inc(S(f"ta_xin{t.par}"), 16)
                    sp.dma_start(k.h[:, t.t, :], k.io["x"][t.t, ::2, :]).then_inc(S(f"ta_xin{t.par}"), 16)
            steps(sp, body, TILES, DEPTH, FIRST)
            sp.wait_ge(S("tables_set"), 32)

        @block.tensor
        def _(pe):
            def body(at):
                if t := at(0):
                    pe.wait_ge(S(f"ta_xin{t.par}"), t.lap() * 32 + 32)
                    t.before(pe, S("ta_xT"), 2)
                    for c in range(KD):
                        mm = pe.transpose(bank[t.par][:, c * P:(c + 1) * P], xin[:, t.par, c * P:(c + 1) * P], k.ident[:])
                    mm.then_inc(S("ta_xT_turned"), 1)
                if t := at(1):
                    t.made(pe, S("ta_xT"))
                    t.before(pe, S("ta_probs"), 2)
                    for c in range(KD):
                        mm = pe.matmul(bank[2 + t.par][:, 0:P], xT[:, t.par, c], xT[:, t.par, c], start=c == 0, stop=c == KD - 1)
                    mm.then_inc(S("ta_scores"), 1)
                if t := at(2):
                    t.made(pe, S("ta_probs"))
                    t.before(pe, S("ta_pT"), 2)
                    pe.transpose(bank[4 + t.par][:, 0:P], probs[:, t.par], k.ident[:]).then_inc(S("ta_pT_turned"), 1)
                if t := at(3):
                    t.made(pe, S("ta_pT"))
                    t.before(pe, S("ta_h"), 2)
                    pe.matmul(bank[6 + t.par][:, 0:D], pT[:, t.par], k.h[:, t.t, :], start=True, stop=True).then_inc(S("ta_out"), 1)
            steps(pe, body, TILES, DEPTH, FIRST)

        @block.scalar
        def _(act):
            act.dma_start(k.wqkv[:], k.io["wqkv"]).then_inc(S("weights_loaded"), 16)
            act.dma_start(k.bqk[:], k.io["bqk"]).then_inc(S("weights_loaded"), 16)
            act.dma_start(k.bv[:], k.io["bv"].partition_broadcast(P)).then_inc(S("weights_loaded"), 16)
            act.dma_start(k.gate_bf[:], k.io["gate"]).then_inc(S("weights_loaded"), 16)
            act.dma_start(k.bias[:], k.io["bias"].partition_broadcast(P)).then_inc(S("weights_loaded"), 16)
            act.dma_start(k.router[:], k.io["router"]).then_inc(S("weights_loaded"), 16)
            act.dma_start(k.wqkv1[:], k.io["wqkv1"]).then_inc(S("weights_loaded"), 16)
            act.dma_start(k.shared_bf[:], k.io["shared"]).then_inc(S("weights_loaded"), 16)
            act.preload_act_table(ACT.Exp)

            def body(at):
                if t := at(0):
                    t.made(act, S("ta_xT_turned"))
                    t.before(act, S("ta_scores"), 2)
                    act.copy(xT[:, t.par].rearrange("p c q -> p (c q)"), bank[t.par][:, 0:D]).then_inc(S("ta_xT"), 1)
                if t := at(1):
                    t.made(act, S("ta_shift"))
                    t.before(act, S("ta_pT_turned"), 2)
                    act.activation(probs[:, t.par], bank[2 + t.par][:, 0:P], ACT.Exp, bias=shift[:, t.par:t.par + 1],
                                   scale=scale, accum_out=total[:, t.par:t.par + 1]).then_inc(S("ta_probs"), 1)
            steps(act, body, TILES, DEPTH, FIRST)

        @block.vector
        def _(dve):
            def body(at):
                if t := at(3):
                    t.made(dve, S("ta_probs"))
                    t.before(dve, S("ta_h"), 2)
                    dve.reciprocal(recip[:, t.par:t.par + 1], total[:, t.par:t.par + 1]).then_inc(S("ta_recip"), 1)
                if t := at(1):
                    t.made(dve, S("ta_scores"))
                    t.before(dve, S("ta_shift"), 2)
                    dve.tensor_reduce(mx[:, t.par:t.par + 1], bank[2 + t.par][:, 0:P], AX.X, ALU.max).then_inc(S("ta_max"), 1)
                if t := at(3):
                    t.made(dve, S("ta_recip"))
                    t.made(dve, S("ta_out"))
                    dve.tensor_scalar(k.h[:, t.t, :], bank[6 + t.par][:, 0:D], recip[:, t.par:t.par + 1], None,
                                      ALU.mult).then_inc(S("ta_h"), 1)
                if t := at(1):
                    t.made(dve, S("ta_max"))
                    t.before(dve, S("ta_probs"), 2)
                    dve.tensor_scalar(shift[:, t.par:t.par + 1], mx[:, t.par:t.par + 1], -scale, None,
                                      ALU.mult).then_inc(S("ta_shift"), 1)
                if t := at(3):
                    t.made(dve, S("ta_h"))
                    settle(dve, S("settled_dve"))
                    dve.bn_stats(k.stats[:, t.par], k.h[:, t.t, :]).then_inc(S("ta_stats"), 1)
                if t := at(2):
                    t.made(dve, S("ta_pT_turned"))
                    t.before(dve, S("ta_out"), 2)
                    dve.tensor_copy(pT[:, t.par], bank[4 + t.par][:, 0:P]).then_inc(S("ta_pT"), 1)
                if t := at(3):
                    t.made(dve, S("ta_stats"))
                    settle(dve, S("settled_dve"))
                    dve.bn_aggr(k.agg[:, t.par], k.stats[:, t.par]).then_inc(S("ta_mv"), 1)
                    t.made(dve, S("ta_mv"))
                    dve.tensor_tensor(k.mv[:, t.t, :], k.agg[:, t.par], k.eps[:], ALU.add).then_inc(S("ta_ve"), 1)
            steps(dve, body, TILES, DEPTH, FIRST)
            dve.wait_ge(S("weights_loaded"), 128)
            dve.tensor_copy(k.gate[:], k.gate_bf[:])
            dve.tensor_copy(k.shared[:], k.shared_bf[:])

        @block.gpsimd
        def _(pool):
            with pool.Fori(0, TILES) as t:
                pool.wait_ge(S("ta_ve"), t + 1)
                pool.tensor_tensor(k.rstd[:, bass.ds(t, 1)], k.mv[:, t, 1:2], k.nhalf[:], ALU.pow)


def head_attention(k):
    nc, S = k.nc, k.S
    with ExitStack() as ctx:
        sb = lambda n, s, d: k.sb("ha_" + n, s, d, ctx)
        bank = k.bank
        z, zT = sb("z", [P, 2, D], F32), sb("zT", [P, 2, KD, P], F32)
        q = [sb(f"q{o}", [P, 2, 2, P], F32) for o in range(2)]
        kT = sb("kT", [P, 2, 2, P], F32)
        v = sb("v", [P, 2, HEADS, HEAD + 1], F32)
        bqm = sb("bqm", [P, 2, 2], F32)
        mx, shift = sb("mx", [P, 2, HEADS], F32), sb("shift", [P, 2, HEADS], F32)
        probs = sb("probs", [P, 2, HEADS * P], F32)
        pT = sb("pT", [P, GROUPS, 4 * P], F32)
        recip, o = sb("recip", [P, 2, HEADS, 1], F32), sb("o", [P, 2, D], F32)
        z2, z2T = sb("z2", [P, 2, D], F32), sb("z2T", [P, 2, KD, P], F32)
        eg, s1 = sb("eg", [P, 2, E0], F32), sb("s1", [P, 2, E0], F32)
        gate, biased = sb("gate", [P, 2, E0], F32), sb("biased", [P, 2, E0], F32)
        top, topi = sb("top", [P, 2, 8], F32), sb("topi", [P, 2, 8], U32)
        choice = sb("choice", [P, 2, K0], F32)
        onehot, picked = sb("onehot", [P, 2, K0, E0], F32), sb("picked", [P, 2, K0, E0], F32)
        ranked = sb("ranked", [P, 2, K0, E0], F32)
        chosen = sb("chosen", [P, 2, E0], BF16)
        w, wsum, wr = sb("w", [P, 2, K0], F32), sb("wsum", [P, 2, 2], F32), sb("wr", [P, 2, 1], F32)
        rank, kept = sb("rank", [P, 2, K0], F32), sb("kept", [P, 2, K0], F32)
        slot, slot2 = sb("slot", [P, 2, K0], F32), sb("slot2", [P, 2, K0], F32)
        to = sb("to", [P, 2, K0], U32)
        pay = sb("pay", [P, 2, K0, 2], U32)
        B_ZT, B_Q, B_S, B_PT, B_O, B_K = 0, 1, 2, 4, 6, 7
        DEPTH, FIRST = 5, 8
        scale = HEAD ** -0.5
        wq, wk, wv = (k.wqkv[:, n] for n in range(3))
        block = ctx.enter_context(nc.Block())

        @block.tensor
        def _(pe):
            def scores(t, g):
                b = bank[B_S + g % 2]
                if g >= 2:
                    t.made(pe, S("ha_probs"), 4, g - 1)
                else:
                    t.before(pe, S("ha_probs"), 1, 4, g + 3)
                if g == 0:
                    t.made(pe, S("ha_q"), 2)
                    t.made(pe, S("ha_k"), 2)
                rows = slice(32 * g, 32 * g + 32)
                for n in range(4):
                    mm = pe.matmul(b[:, n * P:(n + 1) * P], q[n % 2][rows, t.par, n // 2], kT[rows, t.par, n // 2],
                                   start=n == 0, stop=False, skip_group_check=True)
                    yield
                mm = pe.matmul(b[:].rearrange("p (n q) -> p n q", n=4), k.ident_bf[:], bc(k.causal[:].unsqueeze(1), [P, 4, P]),
                               start=False, stop=True, skip_group_check=True)
                mm.then_inc(S("ha_scores"), 1)
                yield

            def turn_probs(t, g):
                t.made(pe, S("ha_probs"), 4, g + 1)
                if g >= 2:
                    t.made(pe, S("ha_pT"), 4, g - 1)
                else:
                    t.before(pe, S("ha_pT"), 1, 4, g + 3)
                for n in range(4):
                    c = (4 * g + n) * P
                    mm = pe.transpose(bank[B_PT + g % 2][:, n * P:(n + 1) * P], probs[:, t.par, c:c + P], k.ident[:])
                mm.then_inc(S("ha_pT_turned"), 1)

            def weigh(t, g):
                t.made(pe, S("ha_pT"), 4, g + 1)
                if g == 0:
                    t.made(pe, S("ha_v"))
                    t.before(pe, S("ha_o"), 1)
                for n in range(4):
                    head = 8 * (n // 2) + 2 * g + n % 2
                    mm = pe.matmul(bank[B_O][:, head * (HEAD + 1):(head + 1) * (HEAD + 1)], pT[:, g, n * P:(n + 1) * P],
                                   v[:, t.par, head], start=True, stop=True)
                    if n == 3:
                        mm.then_inc(S("ha_out"), 1)
                    yield

            def values(t):
                t.made(pe, S("ha_k"), 2)
                for d in range(KD):
                    mm = pe.matmul(bank[B_K][:, D:2 * D], zT[:, t.par, d], wv[:, d], start=d == 0, stop=d == KD - 1)
                    if d == KD - 1:
                        mm.then_inc(S("ha_v_projected"), 1)
                    yield

            def weave(dense, sums):
                for j, _ in enumerate(dense):
                    if j:
                        next(sums, None)
                for _ in sums:
                    pass

            def body(at):
                e, f, s, p, r, c_ = (at(n) for n in range(6))

                def dense(g):
                    return scores(s, g) if s else iter(())

                def sums(g):
                    return weigh(p, g) if p else iter(())
                weave(dense(0), iter(()))
                if p:
                    turn_probs(p, 0)
                if f:
                    f.made(pe, S("ha_z"))
                    f.before(pe, S("ha_zT"), 1)
                    if c_:
                        c_.made(pe, S("r0_hi"))
                    for c in range(KD):
                        mm = pe.transpose(bank[B_ZT][:, c * P:(c + 1) * P], z[:, f.par, c * P:(c + 1) * P], k.ident[:])
                    mm.then_inc(S("ha_zT_turned"), 1)
                weave(dense(1), sums(0))
                if p:
                    turn_probs(p, 1)
                if f:
                    f.made(pe, S("ha_zT"))
                    if c_:
                        c_.made(pe, S("r0_eg"))
                    for c in range(2):
                        for d in range(KD):
                            mm = pe.matmul(bank[B_Q][:, c * P:(c + 1) * P], wq[:, d, c * P:(c + 1) * P], zT[:, f.par, d],
                                           start=d == 0, stop=d == KD - 1)
                    mm.then_inc(S("ha_q_projected"), 1)
                weave(dense(2), sums(1))
                if p:
                    turn_probs(p, 2)
                if f:
                    f.before(pe, S("ha_v"), 1)
                    for c in range(2):
                        for d in range(KD):
                            mm = pe.matmul(bank[B_K][:, c * P:(c + 1) * P], wk[:, d, c * P:(c + 1) * P], zT[:, f.par, d],
                                           start=d == 0, stop=d == KD - 1)
                    mm.then_inc(S("ha_k_projected"), 1)
                if c_:
                    c_.made(pe, S("r0_chosen"))
                    c_.before(pe, S("r0_counted"), 1)
                    if f:
                        f.made(pe, S("ha_q"), 2)
                    pe.matmul(bank[B_Q][:, 2 * E0 + D:3 * E0 + D], k.before[:], chosen[:, c_.par], start=True, stop=False)
                    pe.matmul(bank[B_Q][:, 2 * E0 + D:3 * E0 + D], k.ones_bf[:], k.count0[:, c_.par],
                              start=False, stop=True).then_inc(S("r0_ranks"), 1)
                weave(dense(3), sums(2))
                if p:
                    turn_probs(p, 3)
                if r:
                    r.made(pe, S("r0_z2"))
                    if f:
                        f.made(pe, S("ha_zT"))
                    for c in range(KD):
                        mm = pe.transpose(bank[B_ZT][:, c * P:(c + 1) * P], z2[:, r.par, c * P:(c + 1) * P], k.ident[:])
                    mm.then_inc(S("r0_z2T_turned"), 1)
                weave(values(f) if f else iter(()), sums(3))
                if r:
                    r.made(pe, S("r0_z2T"))
                    if f:
                        f.made(pe, S("ha_q"), 2)
                    if c_:
                        c_.made(pe, S("r0_ranked"))
                    for d in range(KD):
                        mm = pe.matmul(bank[B_Q][:, D:D + E0], z2T[:, r.par, d], k.gate[:, d], start=d == 0, stop=d == KD - 1)
                    mm.then_inc(S("r0_logits"), 1)
            steps(pe, body, TILES, DEPTH, FIRST)

        @block.scalar
        def _(act):
            act.preload_act_table(ACT.Exp)

            def copy_probs(t, g):
                t.made(act, S("ha_pT_turned"), 4, g + 1)
                t.before(act, S("ha_out"), 1, 4, g + 1)
                act.copy(pT[:, g], bank[B_PT + g % 2][:]).then_inc(S("ha_pT"), 1)

            def exponentials(t, g):
                t.made(act, S("ha_shift"), 4, g + 1)
                t.before(act, S("ha_pT_turned"), 2, 4, g + 1)
                for n in range(4):
                    c = 4 * g + n
                    e_ = act.activation(probs[:, t.par, c * P:(c + 1) * P], bank[B_S + g % 2][:, n * P:(n + 1) * P], ACT.Exp,
                                        bias=shift[:, t.par, c:c + 1], scale=scale)
                e_.then_inc(S("ha_probs"), 1)

            def body(at):
                e, f, s, p, r, c_ = (at(n) for n in range(6))
                if p:
                    copy_probs(p, 0)
                if f:
                    f.made(act, S("ha_zT_turned"))
                    f.before(act, S("ha_v_projected"), 2)
                    act.copy(zT[:, f.par].rearrange("p c q -> p (c q)"), bank[B_ZT][:, 0:D]).then_inc(S("ha_zT"), 1)
                if s:
                    exponentials(s, 0)
                if p:
                    copy_probs(p, 1)
                if s:
                    exponentials(s, 1)
                if p:
                    copy_probs(p, 2)
                if s:
                    exponentials(s, 2)
                if f:
                    f.made(act, S("ha_k_projected"))
                    f.before(act, S("ha_scores"), 2, 4)
                    for c in range(2):
                        act.activation(kT[:, f.par, c], bank[B_K][:, c * P:(c + 1) * P], ACT.Identity,
                                       bias=k.bqk[:, 1, c:c + 1]).then_inc(S("ha_k"), 1)
                if p:
                    copy_probs(p, 3)
                if r:
                    r.made(act, S("r0_z2T_turned"))
                    r.before(act, S("r0_lo"), 2)
                    act.copy(z2T[:, r.par].rearrange("p c q -> p (c q)"), bank[B_ZT][:, 0:D]).then_inc(S("r0_z2T"), 1)
                    act.copy(k.zhi[:, :, bass.ts(r.t, P)], bank[B_ZT][:, 0:D].rearrange("p (c q) -> p c q", c=KD)
                             ).then_inc(S("r0_hi"), 1)
                if s:
                    exponentials(s, 3)
                if f:
                    f.made(act, S("ha_v_projected"))
                    f.before(act, S("ha_out"), 2, 4)
                    act.copy(v[:, f.par, :, 0:HEAD], bank[B_K][:, D:2 * D].rearrange("p (h e) -> p h e", h=HEADS)
                             ).then_inc(S("ha_v"), 1)
                if r:
                    r.made(act, S("r0_logits"))
                    r.before(act, S("r0_s1"), 2)
                    act.activation(eg[:, r.par], bank[B_Q][:, D:D + E0], ACT.Exp, scale=-1.0).then_inc(S("r0_eg"), 1)
            steps(act, body, TILES, DEPTH, FIRST)

        @block.vector
        def _(dve):
            for par in range(2):
                dve.memset(v[:, par, :, HEAD:HEAD + 1], 1.0)
                for c in range(2):
                    dve.tensor_scalar(bqm[:, par, c:c + 1], k.bqk[:, 0, c:c + 1], k.parity[:, par:par + 1], None, ALU.mult)
            dve.memset(k.count0[:, 0], 0.0).then_inc(S("ha_set"), 1)
            dve.wait_ge(S("ha_set"), 1)

            def shifts(t, g):
                c = slice(4 * g, 4 * g + 4)
                t.made(dve, S("ha_scores"), 4, g + 1)
                t.before(dve, S("ha_shift"), 2, 4, g + 1)
                dve.tensor_reduce(mx[:, t.par, c], bank[B_S + g % 2][:].rearrange("p (n q) -> p n q", n=4), AX.X, ALU.max
                                  ).then_inc(S("ha_max"), 1)
                yield
                t.made(dve, S("ha_max"), 4, g + 1)
                t.before(dve, S("ha_probs"), 2, 4, g + 1)
                dve.tensor_scalar(shift[:, t.par, c], mx[:, t.par, c], -scale, None, ALU.mult).then_inc(S("ha_shift"), 1)
                yield

            def route(r):
                r.made(dve, S("r0_eg"))
                dve.tensor_scalar(s1[:, r.par], eg[:, r.par], 1.0, None, ALU.add).then_inc(S("r0_s1"), 1)
                yield
                r.made(dve, S("r0_s1"))
                dve.reciprocal(gate[:, r.par], s1[:, r.par]).then_inc(S("r0_gate"), 1)
                yield
                r.made(dve, S("r0_gate"))
                dve.tensor_tensor(biased[:, r.par], gate[:, r.par], k.bias[:], ALU.add).then_inc(S("r0_biased"), 1)
                yield
                r.made(dve, S("r0_biased"))
                settle(dve, S("settled_dve"))
                dve.max(top[:, r.par], biased[:, r.par]).then_inc(S("r0_top"), 1)
                yield
                r.made(dve, S("r0_top"))
                settle(dve, S("settled_dve"))
                dve.max_index(topi[:, r.par], top[:, r.par], biased[:, r.par]).then_inc(S("r0_topi"), 1)
                yield
                r.made(dve, S("r0_topi"))
                dve.tensor_copy(choice[:, r.par], topi[:, r.par, 0:K0]).then_inc(S("r0_choice"), 1)
                yield
                r.made(dve, S("r0_choice"))
                dve.tensor_tensor(onehot[:, r.par], bc(k.iota_e[:].unsqueeze(1), [P, K0, E0]),
                                  bc(choice[:, r.par].unsqueeze(2), [P, K0, E0]), ALU.is_equal).then_inc(S("r0_onehot"), 1)
                yield
                r.made(dve, S("r0_onehot"))
                with nc.allow_low_precision("counts of 0 and 1"):
                    dve.tensor_reduce(chosen[:, r.par], onehot[:, r.par].rearrange("p n e -> p e n"), AX.X,
                                      ALU.add).then_inc(S("r0_chosen"), 1)
                yield

            def weights(w_):
                par = w_.par
                w_.made(dve, S("r0_ranks"))
                dve.tensor_tensor(ranked[:, par], onehot[:, par],
                                  bc(bank[B_Q][:, 2 * E0 + D:3 * E0 + D].unsqueeze(1), [P, K0, E0]), ALU.mult
                                  ).then_inc(S("r0_ranked"), 1)
                dve.tensor_tensor(picked[:, par], onehot[:, par], bc(gate[:, par].unsqueeze(1), [P, K0, E0]), ALU.mult
                                  ).then_inc(S("r0_picked"), 1)
                dve.tensor_tensor(k.count0[:, 1 - par], k.count0[:, par], chosen[:, par], ALU.add).then_inc(S("r0_counted"), 1)
                yield
                w_.made(dve, S("r0_ranked"))
                dve.tensor_reduce(rank[:, par], ranked[:, par], AX.X, ALU.add).then_inc(S("r0_rank"), 1)
                w_.made(dve, S("r0_picked"))
                dve.tensor_reduce(w[:, par], picked[:, par], AX.X, ALU.add).then_inc(S("r0_w"), 1)
                yield
                w_.made(dve, S("r0_rank"))
                dve.tensor_scalar(kept[:, par], rank[:, par], float(CAP0), None, ALU.is_lt).then_inc(S("r0_kept"), 1)
                dve.scalar_tensor_tensor(slot[:, par], choice[:, par], float(CAP0), rank[:, par], ALU.mult, ALU.add
                                         ).then_inc(S("r0_slot"), 1)
                w_.made(dve, S("r0_w"))
                dve.tensor_reduce(wsum[:, par, 0:1], w[:, par], AX.X, ALU.add).then_inc(S("r0_wsum"), 1)
                yield
                w_.made(dve, S("r0_slot"))
                w_.made(dve, S("r0_kept"))
                dve.scalar_tensor_tensor(slot2[:, par], slot[:, par], k.trash0[:, 0:1], kept[:, par], ALU.subtract,
                                         ALU.mult).then_inc(S("r0_slot2"), 1)
                w_.made(dve, S("r0_wsum"))
                dve.tensor_scalar(wsum[:, par, 1:2], wsum[:, par, 0:1], 1e-12, None, ALU.max).then_inc(S("r0_clipped"), 1)
                yield
                w_.made(dve, S("r0_slot2"))
                if w_.const >= 2:
                    dve.wait_ge(S(f"r0_scattered{par}"), w_.lap() * 16 * K0)
                dve.tensor_scalar(to[:, par], slot2[:, par], k.trash0[:, 0:1], None, ALU.add).then_inc(S("r0_to"), 1)
                w_.made(dve, S("r0_clipped"))
                dve.reciprocal(wr[:, par], wsum[:, par, 1:2]).then_inc(S("r0_wr"), 1)
                dve.tensor_copy(pay[:, par, :, 0], bc(k.ids[:, bass.ds(w_.t, 1)], [P, K0])).then_inc(S("r0_pay"), 1)
                yield
                w_.made(dve, S("r0_wr"))
                dve.scalar_tensor_tensor(pay[:, par, :, 1].bitcast(F32), w[:, par], wr[:, par], kept[:, par], ALU.mult,
                                         ALU.mult).then_inc(S("r0_pay"), 1)
                yield

            def norm(p):
                par = p.par
                view = bank[B_O][:, 0:HEADS * (HEAD + 1)].rearrange("p (h e) -> p h e", h=HEADS)
                p.made(dve, S("ha_out"), 4)
                dve.reciprocal(recip[:, par], view[:, :, HEAD:HEAD + 1]).then_inc(S("ha_recip"), 1)
                yield
                p.made(dve, S("ha_recip"))
                dve.tensor_tensor(o[:, par].rearrange("p (h e) -> p h e", h=HEADS), view[:, :, 0:HEAD],
                                  bc(recip[:, par], [P, HEADS, HEAD]), ALU.mult).then_inc(S("ha_o"), 1)
                yield
                p.made(dve, S("ha_o"))
                p.made(dve, S("ha_bv"))
                dve.tensor_tensor(k.h[:, p.t, :], k.h[:, p.t, :], o[:, par], ALU.add).then_inc(S("ha_h"), 1)
                yield
                p.made(dve, S("ha_h"))
                settle(dve, S("settled_dve"))
                dve.bn_stats(k.stats[:, par], k.h[:, p.t, :]).then_inc(S("ha_stats"), 1)
                yield
                p.made(dve, S("ha_stats"))
                settle(dve, S("settled_dve"))
                dve.bn_aggr(k.agg[:, par], k.stats[:, par]).then_inc(S("ha_mv"), 1)
                yield
                p.made(dve, S("ha_mv"))
                dve.tensor_tensor(k.mv[:, p.t, :], k.agg[:, par], k.eps[:], ALU.add).then_inc(S("ha_ve"), 1)
                yield

            def body(at):
                e, f, s, p, r, c_ = (at(n) for n in range(6))
                norming = norm(r) if r else iter(())
                routing = route(c_) if c_ else iter(())
                weighing = weights(c_) if c_ else iter(())
                shifting = [shifts(s, g) if s else iter(()) for g in range(4)]
                next(norming, None)
                if e:
                    e.before(dve, S("ha_zT_turned"), 2)
                    dve.tensor_scalar(z[:, e.par], k.h[:, e.t, :], k.mv[:, e.t, 0:1], k.rstd[:, bass.ds(e.t, 1)],
                                      ALU.subtract, ALU.mult).then_inc(S("ha_z"), 1)
                next(norming, None)
                next(routing, None)
                next(shifting[0], None)
                next(norming, None)
                next(shifting[0], None)
                next(routing, None)
                next(norming, None)
                next(routing, None)
                next(norming, None)
                next(routing, None)
                next(norming, None)
                next(shifting[1], None)
                next(routing, None)
                next(shifting[1], None)
                if f:
                    f.made(dve, S("ha_q_projected"))
                    f.before(dve, S("ha_scores"), 2, 4)
                    for o_ in range(2):
                        dve.scalar_tensor_tensor(q[o_][:, f.par], bank[B_Q][:, 0:D].rearrange("p (c q) -> p c q", c=2),
                                                 k.parity[:, o_:o_ + 1],
                                                 bc(bqm[:, o_].unsqueeze(2), [P, 2, P]), ALU.mult, ALU.add
                                                 ).then_inc(S("ha_q"), 1)
                        next(routing, None)
                if r:
                    r.made(dve, S("ha_rstd"))
                    if r.const >= 2:
                        dve.wait_ge(S(f"r0_stored{r.par}"), r.lap() * 16)
                    dve.tensor_scalar(z2[:, r.par], k.h[:, r.t, :], k.mv[:, r.t, 0:1], k.rstd[:, bass.ds(r.t, 1)],
                                      ALU.subtract, ALU.mult).then_inc(S("r0_z2"), 1)
                for _ in routing:
                    pass
                for _ in shifting[2]:
                    pass
                next(weighing, None)
                next(weighing, None)
                for _ in shifting[3]:
                    next(weighing, None)
                for _ in weighing:
                    pass
                if r:
                    r.made(dve, S("r0_hi"))
                    dve.tensor_tensor(k.zlo[:, :, bass.ts(r.t, P)], z2T[:, r.par],
                                      k.zhi[:, :, bass.ts(r.t, P)].bitcast(F32), ALU.subtract
                                      ).then_inc(S("r0_lo"), 1)
            steps(dve, body, TILES, DEPTH, FIRST)

        @block.gpsimd
        def _(pool):
            def body(at):
                f, r, c_ = at(1), at(4), at(5)
                if f:
                    f.made(pool, S("ha_z"))
                    pool.tensor_tensor(k.h[:, f.t, :], k.h[:, f.t, :], k.bv[:], ALU.add).then_inc(S("ha_bv"), 1)
                if r:
                    r.made(pool, S("ha_ve"))
                    pool.tensor_tensor(k.rstd[:, bass.ds(r.t, 1)], k.mv[:, r.t, 1:2], k.nhalf[:], ALU.pow
                                       ).then_inc(S("ha_rstd"), 1)
                if c_:
                    c_.made(pool, S("r0_to"))
                    c_.made(pool, S("r0_pay"), 2)
                    settle(pool, S("settled_pool"))
                    for n in range(K0):
                        pool.indirect_dma_start(out=k.table0, out_offset=bass.IndirectOffsetOnAxis(ap=to[:, c_.par, n:n + 1], axis=0),
                                                in_=pay[:, c_.par, n, :], in_offset=None, bounds_check=E0 * CAP0 - 1,
                                                oob_is_err=False).then_inc(S(f"r0_scattered{c_.par}"), 16)
            steps(pool, body, TILES, DEPTH, FIRST)
            for par in range(2):
                pool.wait_ge(S(f"r0_scattered{par}"), 16 * K0 * TILES // 2)

        @block.sync
        def _(sp):
            def body(at):
                if r := at(4):
                    r.made(sp, S("r0_z2"))
                    sp.dma_start(k.z0[bass.ts(r.t, P), :], z2[:, r.par]).then_inc(S(f"r0_stored{r.par}"), 16)
            for rows in (k.acc[0:TOKENS, :], k.z0[TOKENS:, :], k.z1[TOKENS:, :], k.out[TOKENS:, :]):
                view = rows.rearrange("(c p) d -> p c d", p=P)
                sp.dma_start(view, bc(k.zeros[:].unsqueeze(1), view.shape)).then_inc(S("zero_rows_set"), 16)
            steps(sp, body, TILES, DEPTH, FIRST)
            sp.wait_ge(S("zero_rows_set"), 64)
            for par in range(2):
                sp.wait_ge(S(f"r0_stored{par}"), 16 * TILES // 2)


def first_mixture(k):
    nc, S = k.nc, k.S
    TURN, SC = 4, CAP0 // P
    AHEAD = TURN - 1
    SG = 512 // P
    with ExitStack() as ctx:
        sb = lambda n, s, d: k.sb("m0_" + n, s, d, ctx)
        bank = k.bank
        shared = k.shared
        sgs, hfs = sb("sgs", [P, 2, 512], F32), sb("hfs", [P, 2, 512], F32)
        hhs, hls = sb("hhs", [P, 2, 512], F32R), sb("hls", [P, 2, 512], F32R)
        active, upto, idle = sb("active", [P, E0], F32), sb("upto", [P, E0], F32), sb("idle", [P, E0], F32)
        place, place2 = sb("place", [P, E0], F32), sb("place2", [P, E0], F32)
        is_at, named = sb("is_at", [P, E0, E0], F32), sb("named", [P, E0, E0], F32)
        order, turns = sb("order", [P, E0 + TURN], I32), sb("turns", [P, 1], I32)
        up3, up3i, tsh = sb("up3", [P, 1], F32), sb("up3i", [P, 1], I32), sb("zero_e", [P, E0], F32)
        source = sb("source", [P, TURN, SC, 2], U32)
        slots = sb("slots", [P, TURN, SC, 2], U32)
        x = sb("x", [P, TURN, SC, D], F32)
        raw, wts = sb("raw", [P, 2, 3 * D], BF16), sb("wts", [P, 2, 3 * D], F32R)
        xh, xl = sb("xh", [P, 2, KD, CAP0], F32R), sb("xl", [P, 2, KD, CAP0], F32R)
        sg, hf = sb("sg", [P, 2, CAP0], F32), sb("hf", [P, 2, CAP0], F32)
        hh, hl = sb("hh", [P, 2, CAP0], F32R), sb("hl", [P, 2, CAP0], F32R)
        yw = sb("yw", [P, TURN, SC, D], F32)
        B_X, B_H, B_Y, B_C = 0, 2, 4, 7
        table_rows = k.table0[0:E0 * CAP0, :].rearrange("(e c p) w -> e p c w", e=E0, p=P)
        top_e = E0 - 1
        block = ctx.enter_context(nc.Block())

        def w13(t, n, c):
            return t[..., (2 * n + c) * P:(2 * n + c + 1) * P]

        @block.sync
        def _(sp):
            sp.wait_ge(S("m0_listed"), 2)
            count = sp.value_load(turns[0:1, 0:1], min_val=1, max_val=E0 // TURN)

            def expert(at):
                return sp.value_load(order[0:1, at], min_val=0, max_val=top_e)

            def rows(e, v):
                sp.dma_start(source[:, v], table_rows[e]).then_inc(S(f"m0_source{v}"), 16)

            def weights(e, u):
                sp.dma_start(raw[:, u], k.io["moe0"][e]).then_inc(S(f"m0_raw{u}"), 16)

            def table(e, v):
                sp.dma_start(slots[:, v], table_rows[e]).then_inc(S(f"m0_slots{v}"), 16)
            for v in range(TURN):
                e = expert(slice(v, v + 1))
                rows(e, v)
                if v < 2:
                    weights(e, v)
                    table(e, v)
            for v in range(2):
                sp.wait_ge(S("m0_cast"), v + 1)
                weights(expert(slice(v + 2, v + 3)), v)
            with sp.Fori(0, count) as i:
                for pair in range(TURN // 2):
                    both = [(i * TURN + v, v % 2, v) for v in (2 * pair, 2 * pair + 1)]
                    for m, u, v in both:
                        sp.wait_ge(S("m0_x_turned"), m + 1)
                        settle(sp, S("settled_sp"))
                        rows(expert(bass.ds(m + TURN, 1)), v)
                    for m, u, v in both:
                        sp.wait_ge(S("m0_added"), (m + 1) * 16 * SC)
                        settle(sp, S("settled_sp"))
                        table(expert(bass.ds(m + 2, 1)), (v + 2) % TURN)
                    for m, u, v in both:
                        sp.wait_ge(S("m0_cast"), m + 3)
                        settle(sp, S("settled_sp"))
                        weights(expert(bass.ds(m + TURN, 1)), u)
            for u in range(2):
                sp.wait_ge(S(f"m0_raw{u}"), (count * 2 + 2) * 16)
                settle(sp, S("settled_sp"))
            for v in range(TURN):
                sp.wait_ge(S(f"m0_source{v}"), (count + 1) * 16)
                settle(sp, S("settled_sp"))
                sp.wait_ge(S(f"m0_slots{v}"), (count + (v < 2)) * 16)
                settle(sp, S("settled_sp"))

        @block.gpsimd
        def _(pool):
            pool.wait_ge(S("m0_listed"), 2)
            count = pool.value_load(turns[0:1, 0:1], min_val=1, max_val=E0 // TURN)

            def gather(v):
                for c in range(SC):
                    pool.indirect_dma_start(out=x[:, v, c, :], out_offset=None, in_=k.z0,
                                            in_offset=bass.IndirectOffsetOnAxis(ap=source[:, v, c, 0:1], axis=0)
                                            ).then_inc(S(f"m0_x{v}"), 16)
            half = PAD0 // (2 * SC)
            for c in range(2 * SC):
                pool.dma_start(k.acc[TOKENS + c * half:TOKENS + (c + 1) * half, :], k.zeros[0:half]
                               ).then_inc(S("m0_added"), 16)
            for v in range(AHEAD):
                pool.wait_ge(S(f"m0_source{v}"), 16)
                gather(v)
            with pool.Fori(0, count) as i:
                for v in range(TURN):
                    m, ahead = i * TURN + v, (v + AHEAD) % TURN
                    pool.wait_ge(S(f"m0_source{ahead}"), (i + (v + AHEAD) // TURN) * 16 + 16)
                    settle(pool, S("settled_pool"))
                    gather(ahead)
                    pool.wait_ge(S("m0_added"), (m + 2) * 16 * SC)
                    pool.wait_ge(S(f"m0_slots{v}"), i * 16 + 16)
                    pool.wait_ge(S("m0_y_weighted"), m * SC + SC)
                    settle(pool, S("settled_pool"))
                    for c in range(SC):
                        pool.indirect_dma_start(out=k.acc, out_offset=bass.IndirectOffsetOnAxis(ap=slots[:, v, c, 0:1], axis=0),
                                                in_=yw[:, v, c, :], in_offset=None, compute_op=ALU.add
                                                ).then_inc(S("m0_added"), 16)
            for v in range(TURN):
                pool.wait_ge(S(f"m0_x{v}"), (count + (v < AHEAD)) * (16 * SC))
            pool.wait_ge(S("m0_added"), count * (16 * SC * TURN) + 32 * SC)

        @block.tensor
        def _(pe):
            pe.matmul(bank[B_C][:, 0:E0], k.ones_bf[:], k.count0[:, 0], start=True, stop=True).then_inc(S("m0_counted"), 1)

            def shared_hidden(g):
                for n in range(2):
                    if g >= 2:
                        pe.wait_ge(S("m0s_hf"), g - 1)
                    for j, (part, c) in enumerate((a, b) for a in (k.zhi, k.zlo) for b in range(KD)):
                        mm = pe.matmul(bank[2 * (g % 2) + n][:], w13(shared, n, c), part[:, c, g * 512:(g + 1) * 512],
                                       start=j == 0, stop=j == 2 * KD - 1)
                mm.then_inc(S("m0s_h"), 1)

            def shared_out(g):
                pe.wait_ge(S("m0s_hl"), g + 1)
                for c in range(SG):
                    if c % 2 == 0 and g:
                        pe.wait_ge(S("m0s_added"), 2 * g - 1 + c // 2)
                    for part, first in ((hhs, True), (hls, False)):
                        mm = pe.matmul(bank[4 + c // 2][:, c % 2 * D:(c % 2 + 1) * D], part[:, g % 2, c * P:(c + 1) * P],
                                       shared[:, 2 * D:3 * D], start=first, stop=not first)
                    if c % 2:
                        mm.then_inc(S("m0s_y"), 1)
            for g in range(TILES // SG + 1):
                if g < TILES // SG:
                    shared_hidden(g)
                if g:
                    shared_out(g - 1)
            pe.wait_ge(S("m0s_added"), 2 * TILES // SG)
            pe.wait_ge(S("m0_listed"), 2)
            count = pe.value_load(turns[0:1, 0:1], min_val=1, max_val=E0 // TURN)

            def turn(v, u, lap):
                pe.wait_ge(S(f"m0_x{v}"), lap * 16 * SC + 16 * SC)
                for d in range(KD):
                    for c in range(SC):
                        mm = pe.transpose(bank[B_X + u][:, d * CAP0 + c * P:d * CAP0 + (c + 1) * P],
                                          x[:, v, c, d * P:(d + 1) * P], k.ident[:])
                mm.then_inc(S("m0_x_turned"), 1)
            for v in range(2):
                turn(v, v, 0)
            with pe.Fori(0, count) as i:
                for pair in range(TURN // 2):
                    both = [(i * TURN + v, v % 2, v) for v in (2 * pair, 2 * pair + 1)]
                    for m, u, v in both:
                        pe.wait_ge(S("m0_cast"), m + 1)
                        pe.wait_ge(S("m0_xl"), m + 1)
                        for n in range(2):
                            for j, (part, d) in enumerate((a, b) for a in (xh, xl) for b in range(KD)):
                                mm = pe.matmul(bank[B_H + u][:, n * CAP0:(n + 1) * CAP0], w13(wts[:, u], n, d), part[:, u, d],
                                               start=j == 0, stop=j == 2 * KD - 1)
                        mm.then_inc(S("m0_h"), 1)
                    if pair:
                        pe.wait_ge(S("m0_y_weighted"), (i * TURN + 2) * SC)
                    for m, u, v in both:
                        pe.wait_ge(S("m0_hl"), m + 1)
                        for c in range(SC):
                            for part, first in ((hh, True), (hl, False)):
                                mm = pe.matmul(bank[B_Y + u][:, c * D:(c + 1) * D], part[:, u, c * P:(c + 1) * P],
                                               wts[:, u, 2 * D:3 * D], start=first, stop=not first)
                        mm.then_inc(S("m0_y"), 1)
                    for m, u, v in both:
                        turn((v + 2) % TURN, u, i + (v + 2) // TURN)
                pe.wait_ge(S("m0_y_weighted"), (i * TURN + TURN) * SC)

        @block.scalar
        def _(act):
            act.preload_act_table(ACT.Silu)
            for g in range(TILES // SG):
                act.wait_ge(S("m0s_h"), g + 1)
                if g >= 2:
                    act.wait_ge(S("m0s_hf"), g - 1)
                act.activation(sgs[:, g % 2], bank[2 * (g % 2)][:], ACT.Silu).then_inc(S("m0s_sg"), 1)

            act.wait_ge(S("m0_listed"), 2)
            count = act.value_load(turns[0:1, 0:1], min_val=1, max_val=E0 // TURN)

            def upper(m, u):
                act.wait_ge(S("m0_x_turned"), m + 1)
                act.copy(xh[:, u].rearrange("p d s -> p (d s)"), bank[B_X + u][:]).then_inc(S("m0_xh"), 1)
            for v in range(2):
                upper(v, v)
            with act.Fori(0, count) as i:
                for pair in range(TURN // 2):
                    both = [(i * TURN + v, v % 2, v) for v in (2 * pair, 2 * pair + 1)]
                    for m, u, v in both:
                        act.wait_ge(S("m0_h"), m + 1)
                        act.activation(sg[:, u], bank[B_H + u][:, 0:CAP0], ACT.Silu).then_inc(S("m0_sg"), 1)
                    for m, u, v in both:
                        act.wait_ge(S("m0_y"), m + 1)
                        act.wait_ge(S(f"m0_slots{v}"), i * 16 + 16)
                        for c in range(SC):
                            act.activation(yw[:, v, c], bank[B_Y + u][:, c * D:(c + 1) * D], ACT.Copy,
                                           scale=slots[:, v, c, 1:2].bitcast(F32)).then_inc(S("m0_y_weighted"), 1)
                    for m, u, v in both:
                        upper(m + 2, u)

        @block.vector
        def _(dve):
            def chain(ins, n):
                ins.then_inc(S("m0_list_steps"), 1)
                dve.wait_ge(S("m0_list_steps"), n)
            dve.memset(order[:], 0).then_inc(S("m0_order_set"), 1)
            dve.memset(tsh[:], 0.0).then_inc(S("m0_order_set"), 1)
            dve.wait_ge(S("m0_order_set"), 2)
            dve.wait_ge(S("m0_counted"), 1)
            chain(dve.tensor_scalar(active[:], bank[B_C][:, 0:E0], 0.0, None, ALU.is_gt), 1)
            chain(dve.tensor_tensor_scan(upto[:], active[:], tsh[:], 0.0, ALU.add, ALU.add), 2)
            chain(dve.tensor_scalar(idle[:], k.iota_e[:], upto[:, E0 - 1:E0], None, ALU.add), 3)
            chain(dve.tensor_tensor(idle[:], idle[:], upto[:], ALU.subtract), 4)
            chain(dve.scalar_tensor_tensor(place[:], upto[:], -1.0, idle[:], ALU.add, ALU.subtract), 5)
            chain(dve.tensor_tensor(place2[:], place[:], active[:], ALU.mult), 6)
            chain(dve.tensor_tensor(place[:], place2[:], idle[:], ALU.add), 7)
            chain(dve.tensor_tensor(is_at[:], bc(k.iota_e[:].unsqueeze(2), [P, E0, E0]), bc(place[:].unsqueeze(1), [P, E0, E0]),
                                    ALU.is_equal), 8)
            chain(dve.tensor_tensor(named[:], is_at[:], bc(k.iota_e[:].unsqueeze(1), [P, E0, E0]), ALU.mult), 9)
            with nc.allow_low_precision("numbers of experts"):
                dve.tensor_reduce(order[:, 0:E0], named[:], AX.X, ALU.add).then_inc(S("m0_listed"), 1)
            chain(dve.tensor_scalar(up3[:], upto[:, E0 - 1:E0], float(TURN - 1), None, ALU.add), 10)
            chain(dve.tensor_copy(up3i[:], up3[:]), 11)
            dve.tensor_scalar(turns[:], up3i[:], TURN.bit_length() - 1, None, ALU.logical_shift_right).then_inc(S("m0_listed"), 1)
            for g in range(TILES // SG + 1):
                if g < TILES // SG:
                    dve.wait_ge(S("m0s_sg"), g + 1)
                    dve.tensor_tensor(hfs[:, g % 2], sgs[:, g % 2], bank[2 * (g % 2) + 1][:], ALU.mult).then_inc(S("m0s_hf"), 1)
                    dve.wait_ge(S("m0s_hf"), g + 1)
                    dve.tensor_copy(hhs[:, g % 2], hfs[:, g % 2]).then_inc(S("m0s_hh"), 1)
                    dve.wait_ge(S("m0s_hh"), g + 1)
                    dve.tensor_tensor(hls[:, g % 2], hfs[:, g % 2], hhs[:, g % 2].bitcast(F32), ALU.subtract
                                      ).then_inc(S("m0s_hl"), 1)
                if g:
                    for c in range(SG // 2):
                        dve.wait_ge(S("m0s_y"), 2 * (g - 1) + c + 1)
                        rows = k.h[:, (g - 1) * SG + 2 * c:(g - 1) * SG + 2 * c + 2, :].rearrange("p t d -> p (t d)")
                        dve.tensor_tensor(rows, rows, bank[4 + c][:], ALU.add).then_inc(S("m0s_added"), 1)
            dve.wait_ge(S("m0_listed"), 2)
            count = dve.value_load(turns[0:1, 0:1], min_val=1, max_val=E0 // TURN)
            for u in range(2):
                dve.wait_ge(S(f"m0_raw{u}"), 16)
                dve.tensor_copy(wts[:, u], raw[:, u]).then_inc(S("m0_cast"), 1)

            def lower(m, u):
                dve.wait_ge(S("m0_xh"), m + 1)
                dve.tensor_tensor(xl[:, u].rearrange("p d s -> p (d s)"), bank[B_X + u][:],
                                  xh[:, u].rearrange("p d s -> p (d s)").bitcast(F32), ALU.subtract
                                  ).then_inc(S("m0_xl"), 1)
            for v in range(2):
                lower(v, v)
            with dve.Fori(0, count) as i:
                for pair in range(TURN // 2):
                    both = [(i * TURN + v, v % 2, v) for v in (2 * pair, 2 * pair + 1)]
                    for m, u, v in both:
                        dve.wait_ge(S("m0_sg"), m + 1)
                        dve.tensor_tensor(hf[:, u], sg[:, u], bank[B_H + u][:, CAP0:2 * CAP0], ALU.mult).then_inc(S("m0_hf"), 1)
                        dve.wait_ge(S("m0_hf"), m + 1)
                        dve.tensor_copy(hh[:, u], hf[:, u]).then_inc(S("m0_hh"), 1)
                        dve.wait_ge(S("m0_hh"), m + 1)
                        dve.tensor_tensor(hl[:, u], hf[:, u], hh[:, u].bitcast(F32), ALU.subtract).then_inc(S("m0_hl"), 1)
                    for m, u, v in both:
                        dve.wait_ge(S("m0_y"), m + 1)
                        dve.wait_ge(S(f"m0_raw{u}"), (i * 2 + v // 2 + 1) * 16 + 16)
                        dve.tensor_copy(wts[:, u], raw[:, u]).then_inc(S("m0_cast"), 1)
                    for m, u, v in both:
                        lower(m + 2, u)


def last_attention(k):
    nc, S = k.nc, k.S
    with ExitStack() as ctx:
        sb = lambda n, s, d: k.sb("la_" + n, s, d, ctx)
        bank = k.bank
        ac = sb("ac", [P, 2, D], F32)
        z, zT = sb("z", [P, 2, D], F32), sb("zT", [P, 2, KD, P], F32)
        qk, v = sb("qk", [P, 2, 2, KD, P], F32), sb("v", [P, 2, D], F32)
        mx, shift = sb("mx", [P, 2], F32), sb("shift", [P, 2], F32)
        probs, total, recip = sb("probs", [P, 2, P], F32), sb("total", [P, 2], F32), sb("recip", [P, 2], F32)
        pT = sb("pT", [P, 2, P], F32)
        z3, z3T = sb("z3", [P, 2, D], F32), sb("z3T", [P, 2, KD, P], F32)
        base = sb("base", [P, 2, D], F32)
        statsa, agga = sb("statsa", [P, 2, 6], F32), sb("agga", [P, 2, 2], F32)
        lmax, centred, ex = sb("lmax", [P, 2, 1], F32), sb("centred", [P, 2, E1], F32), sb("ex", [P, 2, E1], F32)
        esum, erecip, prob = sb("esum", [P, 2, 1], F32), sb("erecip", [P, 2, 1], F32), sb("prob", [P, 2, E1], F32)
        top, topi = sb("top", [P, 2, 8], F32), sb("topi", [P, 2, 8], U32)
        choice, onehot = sb("choice", [P, 2, K1], F32), sb("onehot", [P, 2, K1, E1], F32)
        chosen, both = sb("chosen", [P, 2, E1], BF16), sb("both", [P, E1], BF16)
        ranked, rank = sb("ranked", [P, 2, K1, E1], F32), sb("rank", [P, 2, K1], F32)
        kept, slot, slot2 = sb("kept", [P, 2, K1], F32), sb("slot", [P, 2, K1], F32), sb("slot2", [P, 2, K1], F32)
        wsum, wr = sb("wsum", [P, 2, 1], F32), sb("wr", [P, 2, 1], F32)
        to, pay = sb("to", [P, 2, K1], U32), sb("pay", [P, 2, K1, 2], U32)
        B_ZT, B_QK, B_V, B_S, B_PT, B_O, B_Z3T, B_R = range(8)
        LOGITS, RANKS = slice(0, 2 * E1), slice(2 * E1, 4 * E1)
        DEPTH, FIRST = 6, 8
        scale = D ** -0.5
        block = ctx.enter_context(nc.Block())

        def pair(t):
            return Pair(t.loop, t.const) if t and t.par else None

        @block.sync
        def _(sp):
            for n in range(2):
                sp.dma_start(k.raw[n][:], k.io[f"w{n + 1}"][0]).then_inc(S(f"m1_raw{n + 1}"), 16)

            def body(at):
                if a := at(0):
                    a.before(sp, S("la_added"), 2)
                    sp.dma_start(ac[:, a.par], k.acc[bass.ts(a.t, P), :]).then_inc(S(f"la_ac{a.par}"), 16)
                if r := at(5):
                    r.made(sp, S("la_z3"))
                    sp.dma_start(k.z1[bass.ts(r.t, P), :], z3[:, r.par]).then_inc(S(f"la_stored{r.par}"), 16)
                    r.made(sp, S("la_base"))
                    sp.dma_start(k.out[bass.ts(r.t, P), :], base[:, r.par]).then_inc(S(f"la_out{r.par}"), 16)
            steps(sp, body, TILES, DEPTH, FIRST)
            for par in range(2):
                sp.wait_ge(S(f"la_stored{par}"), 16 * TILES // 2)
                sp.wait_ge(S(f"la_out{par}"), 16 * TILES // 2)

        @block.tensor
        def _(pe):
            def body(at):
                f, s, p, r = (at(n) for n in range(1, 5))
                rr, ww = pair(r), pair(at(6))
                if s:
                    s.made(pe, S("la_qk"))
                    s.before(pe, S("la_probs"), 1)
                    for c in range(KD):
                        pe.matmul(bank[B_S][:, 0:P], qk[:, s.par, 0, c], qk[:, s.par, 1, c], start=c == 0, stop=False)
                    pe.matmul(bank[B_S][:, 0:P], k.ident_bf[:], k.causal[:], start=False, stop=True
                              ).then_inc(S("la_scores"), 1)
                if p:
                    p.made(pe, S("la_probs"))
                    p.before(pe, S("la_pT"), 1)
                    pe.transpose(bank[B_PT][:, 0:P], probs[:, p.par], k.ident[:]).then_inc(S("la_pT_turned"), 1)
                if f:
                    f.made(pe, S("la_z"))
                    f.before(pe, S("la_zT"), 1)
                    for c in range(KD):
                        mm = pe.transpose(bank[B_ZT][:, c * P:(c + 1) * P], z[:, f.par, c * P:(c + 1) * P], k.ident[:])
                    mm.then_inc(S("la_zT_turned"), 1)
                if ww:
                    ww.made(pe, S("r1_chosen"))
                    ww.before(pe, S("r1_counted"), 1)
                    pe.matmul(bank[B_R][:, RANKS], k.before[:], chosen[:].rearrange("p t e -> p (t e)"), start=True, stop=False)
                    pe.matmul(bank[B_R][:, RANKS.start + E1:RANKS.stop], k.ones_bf[:], chosen[:, 0], start=False, stop=False)
                    pe.matmul(bank[B_R][:, RANKS].rearrange("p (t e) -> p t e", t=2), k.ones_bf[:],
                              bc(k.count1[:].unsqueeze(1), [P, 2, E1]), start=False, stop=True).then_inc(S("r1_ranks"), 1)
                if p:
                    p.made(pe, S("la_pT"))
                    p.made(pe, S("la_v"))
                    p.before(pe, S("la_h"), 1)
                    pe.matmul(bank[B_O][:, 0:D], pT[:, p.par], v[:, p.par], start=True, stop=True).then_inc(S("la_o"), 1)
                if f:
                    f.made(pe, S("la_zT"))
                    f.before(pe, S("la_qk"), 1)
                    for n in range(2):
                        for c in range(2):
                            for d in range(KD):
                                mm = pe.matmul(bank[B_QK][:, (2 * n + c) * P:(2 * n + c + 1) * P],
                                               k.wqkv1[:, n, d, c * P:(c + 1) * P], zT[:, f.par, d],
                                               start=d == 0, stop=d == KD - 1)
                    mm.then_inc(S("la_qk_projected"), 1)
                if r:
                    r.made(pe, S("la_z3"))
                    r.before(pe, S("la_z3T"), 1)
                    for c in range(KD):
                        mm = pe.transpose(bank[B_Z3T][:, c * P:(c + 1) * P], z3[:, r.par, c * P:(c + 1) * P], k.ident[:])
                    mm.then_inc(S("la_z3T_turned"), 1)
                if f:
                    f.before(pe, S("la_v"), 1)
                    for d in range(KD):
                        mm = pe.matmul(bank[B_V][:, 0:D], zT[:, f.par, d], k.wqkv1[:, 2, d], start=d == 0, stop=d == KD - 1)
                    mm.then_inc(S("la_v_projected"), 1)
                if r:
                    r.made(pe, S("la_z3T"))
                    Pair(r.loop, r.const).before(pe, S("r1_ranked" if rr else "r1_centred"), 1)
                    for d in range(KD):
                        mm = pe.matmul(bank[B_R][:, r.par * E1:(r.par + 1) * E1], z3T[:, r.par, d], k.router[:, d],
                                       start=d == 0, stop=d == KD - 1)
                    mm.then_inc(S("la_logits"), 1)
            steps(pe, body, TILES, DEPTH, FIRST)

        @block.scalar
        def _(act):
            act.preload_act_table(ACT.Exp)

            def body(at):
                f, s, p, r, cc = at(1), at(2), at(3), at(4), pair(at(5))
                if p:
                    p.made(act, S("la_pT_turned"))
                    p.before(act, S("la_o"), 2)
                    act.copy(pT[:, p.par], bank[B_PT][:, 0:P]).then_inc(S("la_pT"), 1)
                if f:
                    f.made(act, S("la_zT_turned"))
                    f.before(act, S("la_v_projected"), 2)
                    act.copy(zT[:, f.par].rearrange("p c q -> p (c q)"), bank[B_ZT][:, 0:D]).then_inc(S("la_zT"), 1)
                if s:
                    s.made(act, S("la_shift"))
                    s.before(act, S("la_pT_turned"), 2)
                    act.activation(probs[:, s.par], bank[B_S][:, 0:P], ACT.Exp, bias=shift[:, s.par:s.par + 1], scale=scale,
                                   accum_out=total[:, s.par:s.par + 1]).then_inc(S("la_probs"), 1)
                if cc:
                    cc.made(act, S("r1_centred"))
                    cc.before(act, S("r1_prob"), 1)
                    act.activation(ex[:], centred[:], ACT.Exp).then_inc(S("r1_ex"), 1)
                if f:
                    f.made(act, S("la_qk_projected"))
                    f.before(act, S("la_scores"), 2)
                    act.copy(qk[:, f.par].rearrange("p n c q -> p (n c q)"), bank[B_QK][:]).then_inc(S("la_qk"), 1)
                if r:
                    r.made(act, S("la_z3T_turned"))
                    r.before(act, S("la_logits"), 2)
                    act.copy(z3T[:, r.par].rearrange("p c q -> p (c q)"), bank[B_Z3T][:, 0:D]).then_inc(S("la_z3T"), 1)
                if f:
                    f.made(act, S("la_v_projected"))
                    f.before(act, S("la_o"), 2)
                    act.copy(v[:, f.par], bank[B_V][:, 0:D]).then_inc(S("la_v"), 1)
            steps(act, body, TILES, DEPTH, FIRST)

        @block.vector
        def _(dve):
            dve.memset(k.count1[:], 0.0).then_inc(S("la_set"), 1)
            dve.wait_ge(S("la_set"), 1)

            def norm(t, tag, stats, agg):
                t.made(dve, S(f"la_{tag}"))
                settle(dve, S("settled_dve"))
                dve.bn_stats(stats[:, t.par], k.h[:, t.t, :]).then_inc(S(f"la_{tag}_stats"), 1)
                yield
                t.made(dve, S(f"la_{tag}_stats"))
                settle(dve, S("settled_dve"))
                dve.bn_aggr(agg[:, t.par], stats[:, t.par]).then_inc(S(f"la_{tag}_mv"), 1)
                yield
                t.made(dve, S(f"la_{tag}_mv"))
                dve.tensor_tensor(k.mv[:, t.t, :], agg[:, t.par], k.eps[:], ALU.add
                                  ).then_inc(S(f"la_{tag}_ve"), 1)
                yield

            def route(rr):
                logits = bank[B_R][:, LOGITS].rearrange("p (t e) -> p t e", t=2)
                rr.made(dve, S("la_logits"), 2)
                dve.tensor_reduce(lmax[:], logits, AX.X, ALU.max).then_inc(S("r1_max"), 1)
                yield
                rr.made(dve, S("r1_max"))
                rr.before(dve, S("r1_ex"), 1)
                dve.tensor_tensor(centred[:], logits, bc(lmax[:], [P, 2, E1]), ALU.subtract).then_inc(S("r1_centred"), 1)
                yield
                rr.made(dve, S("r1_ex"))
                dve.tensor_reduce(esum[:], ex[:], AX.X, ALU.add).then_inc(S("r1_esum"), 1)
                yield
                rr.made(dve, S("r1_esum"))
                dve.reciprocal(erecip[:], esum[:]).then_inc(S("r1_erecip"), 1)
                yield
                rr.made(dve, S("r1_erecip"))
                dve.tensor_tensor(prob[:], ex[:], bc(erecip[:], [P, 2, E1]), ALU.mult).then_inc(S("r1_prob"), 1)
                yield
                rr.made(dve, S("r1_prob"))
                for t in range(2):
                    settle(dve, S("settled_dve"))
                    dve.max(top[:, t], prob[:, t]).then_inc(S("r1_top"), 1)
                    yield
                for t in range(2):
                    rr.made(dve, S("r1_top"), 2, t + 1)
                    settle(dve, S("settled_dve"))
                    dve.max_index(topi[:, t], top[:, t], prob[:, t]).then_inc(S("r1_topi"), 1)
                    yield
                rr.made(dve, S("r1_topi"), 2)
                dve.tensor_copy(choice[:], topi[:, :, 0:K1]).then_inc(S("r1_choice"), 1)
                yield
                rr.made(dve, S("r1_choice"))
                dve.tensor_tensor(onehot[:], bc(k.iota_e[:, 0:E1].unsqueeze(1).unsqueeze(1), [P, 2, K1, E1]),
                                  bc(choice[:].unsqueeze(3), [P, 2, K1, E1]), ALU.is_equal).then_inc(S("r1_onehot"), 1)
                yield
                rr.made(dve, S("r1_onehot"))
                with nc.allow_low_precision("counts of 0 and 1"):
                    dve.tensor_reduce(chosen[:], onehot[:].rearrange("p t n e -> p t e n"), AX.X, ALU.add
                                      ).then_inc(S("r1_chosen"), 1)
                yield
                rr.made(dve, S("r1_chosen"))
                dve.tensor_tensor(both[:], chosen[:, 0], chosen[:, 1], ALU.add).then_inc(S("r1_both"), 1)
                yield

            def weights(ww):
                ww.made(dve, S("r1_ranks"))
                dve.tensor_tensor(ranked[:], onehot[:],
                                  bc(bank[B_R][:, RANKS].rearrange("p (t e) -> p t e", t=2).unsqueeze(2), [P, 2, K1, E1]),
                                  ALU.mult).then_inc(S("r1_ranked"), 1)
                yield
                ww.made(dve, S("r1_both"))
                dve.tensor_tensor(k.count1[:], k.count1[:], both[:], ALU.add).then_inc(S("r1_counted"), 1)
                dve.tensor_reduce(wsum[:], top[:, :, 0:K1], AX.X, ALU.add).then_inc(S("r1_wsum"), 1)
                yield
                ww.made(dve, S("r1_ranked"))
                dve.tensor_reduce(rank[:], ranked[:], AX.X, ALU.add).then_inc(S("r1_rank"), 1)
                yield
                ww.made(dve, S("r1_wsum"))
                dve.reciprocal(wr[:], wsum[:]).then_inc(S("r1_wr"), 1)
                yield
                ww.made(dve, S("r1_rank"))
                dve.tensor_scalar(kept[:], rank[:], float(CAP1), None, ALU.is_lt).then_inc(S("r1_kept"), 1)
                dve.scalar_tensor_tensor(slot[:], choice[:], float(STRIDE1), rank[:], ALU.mult, ALU.add
                                         ).then_inc(S("r1_slot"), 1)
                if ww.const:
                    dve.wait_ge(S("r1_scattered"), ww.t * 32 * K1)
                dve.tensor_copy(pay[:, :, :, 0], bc(k.ids[:, bass.ds(ww.t * 2, 2)].unsqueeze(2), [P, 2, K1])
                                ).then_inc(S("r1_pay"), 1)
                yield
                ww.made(dve, S("r1_kept"))
                ww.made(dve, S("r1_slot"))
                dve.scalar_tensor_tensor(slot2[:], slot[:], k.trash1[:, 0:1], kept[:], ALU.subtract, ALU.mult
                                         ).then_inc(S("r1_slot2"), 1)
                ww.made(dve, S("r1_wr"))
                dve.tensor_tensor(pay[:, :, :, 1].bitcast(F32), top[:, :, 0:K1], bc(wr[:], [P, 2, K1]), ALU.mult
                                  ).then_inc(S("r1_pay"), 1)
                yield
                ww.made(dve, S("r1_slot2"))
                dve.tensor_scalar(to[:], slot2[:], k.trash1[:, 0:1], None, ALU.add).then_inc(S("r1_to"), 1)

            def scored(s):
                s.made(dve, S("la_scores"))
                s.before(dve, S("la_shift"), 2)
                dve.tensor_reduce(mx[:, s.par:s.par + 1], bank[B_S][:, 0:P], AX.X, ALU.max).then_inc(S("la_max"), 1)
                yield
                s.made(dve, S("la_max"))
                s.before(dve, S("la_probs"), 2)
                dve.tensor_scalar(shift[:, s.par:s.par + 1], mx[:, s.par:s.par + 1], -scale, None, ALU.mult
                                  ).then_inc(S("la_shift"), 1)
                yield

            def added(a):
                dve.wait_ge(S(f"la_ac{a.par}"), a.lap() * 16 + 16)
                dve.tensor_tensor(k.h[:, a.t, :], k.h[:, a.t, :], ac[:, a.par], ALU.add).then_inc(S("la_added"), 1)
                yield
                yield from norm(a, "added", statsa, agga)

            def weighed(p):
                p.made(dve, S("la_probs"))
                dve.reciprocal(recip[:, p.par:p.par + 1], total[:, p.par:p.par + 1]).then_inc(S("la_recip"), 1)
                yield
                p.made(dve, S("la_recip"))
                p.made(dve, S("la_o"))
                dve.scalar_tensor_tensor(k.h[:, p.t, :], bank[B_O][:, 0:D], recip[:, p.par:p.par + 1], k.h[:, p.t, :],
                                         ALU.mult, ALU.add).then_inc(S("la_h"), 1)
                yield
                yield from norm(p, "h", k.stats, k.agg)

            def body(at):
                a, f, s, p, r = (at(n) for n in range(5))
                cc, ww = pair(at(5)), pair(at(6))
                routing = route(cc) if cc else weights(ww) if ww else iter(())
                adding, scoring, weighing = (fn(t) if t else iter(()) for fn, t in ((added, a), (scored, s), (weighed, p)))
                if f:
                    f.made(dve, S("la_a_rstd"))
                    f.before(dve, S("la_zT_turned"), 2)
                    dve.tensor_scalar(z[:, f.par], k.h[:, f.t, :], k.mv[:, f.t, 0:1], k.rstd[:, bass.ds(f.t, 1)],
                                      ALU.subtract, ALU.mult).then_inc(S("la_z"), 1)
                next(adding, None)
                next(scoring, None)
                if cc:
                    next(routing, None)
                next(scoring, None)
                next(adding, None)
                if cc:
                    next(routing, None)
                if r:
                    r.made(dve, S("la_h_rstd"))
                    r.before(dve, S("la_base"), 2)
                    if r.const >= 2:
                        dve.wait_ge(S(f"la_stored{r.par}"), r.lap() * 16)
                    dve.tensor_scalar(z3[:, r.par], k.h[:, r.t, :], k.mv[:, r.t, 0:1], k.rstd[:, bass.ds(r.t, 1)],
                                      ALU.subtract, ALU.mult).then_inc(S("la_z3"), 1)
                next(weighing, None)
                next(adding, None)
                next(routing, None)
                next(weighing, None)
                next(adding, None)
                while weighing or routing:
                    weighing = weighing if next(weighing, "end") != "end" else None
                    for _ in range(2):
                        routing = routing if routing and next(routing, "end") != "end" else None
                    if not weighing:
                        for _ in routing or ():
                            pass
                        break
            steps(dve, body, TILES, DEPTH, FIRST)

        @block.gpsimd
        def _(pool):
            def body(at):
                a, p, r, ww = at(0), at(3), at(4), pair(at(6))
                if r:
                    r.made(pool, S("la_z3"))
                    if r.const >= 2:
                        pool.wait_ge(S(f"la_out{r.par}"), r.lap() * 16)
                    pool.tensor_tensor(base[:, r.par], k.h[:, r.t, :], z3[:, r.par], ALU.add).then_inc(S("la_base"), 1)
                for t, tag, made in ((a, "added", "a"), (p, "h", "h")):
                    if t:
                        t.made(pool, S(f"la_{tag}_ve"))
                        pool.tensor_tensor(k.rstd[:, bass.ds(t.t, 1)], k.mv[:, t.t, 1:2], k.nhalf[:], ALU.pow
                                           ).then_inc(S(f"la_{made}_rstd"), 1)
                if ww:
                    ww.made(pool, S("r1_to"))
                    ww.made(pool, S("r1_pay"), 2)
                    settle(pool, S("settled_pool"))
                    for t in range(2):
                        for n in range(K1):
                            pool.indirect_dma_start(out=k.table1, out_offset=bass.IndirectOffsetOnAxis(ap=to[:, t, n:n + 1], axis=0),
                                                    in_=pay[:, t, n, :], in_offset=None, bounds_check=E1 * STRIDE1 - 1,
                                                    oob_is_err=False).then_inc(S("r1_scattered"), 16)
            steps(pool, body, TILES, DEPTH, FIRST)
            pool.wait_ge(S("r1_scattered"), 16 * K1 * TILES)


def second_mixture(k):
    nc, S = k.nc, k.S
    SC = -(-SLOTS1 // P)
    LAST = SLOTS1 - (SC - 1) * P
    HALF = SLOTS1 // 2
    ROUNDS = SC // 2
    ALL = 16 * SC
    with ExitStack() as ctx:
        sb = lambda n, s, d: k.sb("m1_" + n, s, d, ctx)
        bank = k.bank
        slots = sb("slots", [P, 2, SC, 2], U32)
        x = sb("x", [P, 2, SC, D], F32)
        raw = k.raw
        hi = [sb(f"w{n}h", [P, FC1 * D], F32R) for n in (1, 2)]
        lo = [sb(f"w{n}l", [P, FC1 * D], F32R) for n in (1, 2)]
        xh, xl = sb("xh", [P, KD, SLOTS1], F32R), sb("xl", [P, KD, SLOTS1], F32R)
        hf = sb("hf", [P, 2, SLOTS1], F32)
        hh, hl = sb("hh", [P, FC1, SLOTS1], F32R), sb("hl", [P, FC1, SLOTS1], F32R)
        yw = sb("yw", [P, SC, D], F32)
        B_H, B_Y, B_X = 0, 4, 6
        table_rows = k.table1[0:E1 * STRIDE1, :].rearrange("(e c p) w -> e p c w", e=E1, p=P)
        w1 = [t[:].rearrange("p (d f) -> p d f", d=KD) for t in (hi[0], lo[0])]
        w2 = [t[:].rearrange("p (f d) -> p f d", f=FC1) for t in (hi[1], lo[1])]
        DEPTH, FIRST = 1, 2
        block = ctx.enter_context(nc.Block())

        def rows(c):
            return P if c < SC - 1 else LAST

        def turned(r, tile, b):
            n = rows(2 * r) + rows(2 * r + 1)
            return tile[:, :, 2 * r * P:2 * r * P + n], bank[B_X + b][:].rearrange("p (d s) -> p d s", d=KD)[:, :, 0:n]

        @block.sync
        def _(sp):
            def body(at):
                if x_ := at(0):
                    if x_.const:
                        x_.before(sp, S("m1_w1_lo"), 1)
                        sp.dma_start(raw[0][:], k.io["w1"][x_.t]).then_inc(S("m1_raw1"), 16)
                    if x_.const >= 2:
                        sp.wait_ge(S("m1_added"), (x_.t - 1) * ALL)
                    sp.dma_start(slots[:, x_.par], table_rows[x_.t]).then_inc(S(f"m1_slots{x_.par}"), 16)
                    if x_.const:
                        x_.before(sp, S("m1_w2_lo"), 1)
                        sp.dma_start(raw[1][:], k.io["w2"][x_.t]).then_inc(S("m1_raw2"), 16)
            steps(sp, body, E1, DEPTH, FIRST)

        @block.gpsimd
        def _(pool):
            def body(at):
                x_, c_ = at(0), at(1)
                if x_:
                    pool.wait_ge(S(f"m1_slots{x_.par}"), x_.lap() * 16 + 16)
                    x_.before(pool, S("m1_x_turned"), 2, ROUNDS)
                    settle(pool, S("settled_pool"))
                    for c in range(SC):
                        n = rows(c)
                        pool.indirect_dma_start(out=x[0:n, x_.par, c, :], out_offset=None, in_=k.z1,
                                                in_offset=bass.IndirectOffsetOnAxis(ap=slots[0:n, x_.par, c, 0:1], axis=0)
                                                ).then_inc(S(f"m1_x{x_.par}_{c // 2}"), 16)
                if c_:
                    for c in range(SC):
                        n = rows(c)
                        c_.made(pool, S("m1_y_weighted"), SC, c + 1)
                        if c == 0:
                            c_.before(pool, S("m1_added"), 1, ALL)
                        settle(pool, S("settled_pool"))
                        pool.indirect_dma_start(out=k.out, out_offset=bass.IndirectOffsetOnAxis(ap=slots[0:n, c_.par, c, 0:1], axis=0),
                                                in_=yw[0:n, c, :], in_offset=None, compute_op=ALU.add
                                                ).then_inc(S("m1_added"), 16)
            steps(pool, body, E1, DEPTH, FIRST)
            pool.wait_ge(S("m1_added"), E1 * ALL)

        @block.tensor
        def _(pe):
            def hidden(c_):
                c_.made(pe, S("m1_w1_lo"))
                c_.made(pe, S("m1_xl"), ROUNDS)
                for f in range(FC1):
                    if f >= 2:
                        c_.made(pe, S("m1_hf"), FC1, f - 1)
                    else:
                        c_.before(pe, S("m1_hf"), 1, FC1, f + FC1 - 1)
                    passes = [(w1[0], xh), (w1[0], xl), (w1[1], xh)]
                    for j, (w, part) in enumerate(passes):
                        for d in range(KD):
                            for s in range(2):
                                mm = pe.matmul(bank[B_H + 2 * (f % 2) + s][:, 0:HALF], w[:, d, f * P:(f + 1) * P],
                                               part[:, d, s * HALF:(s + 1) * HALF],
                                               start=j == 0 and d == 0, stop=j == len(passes) - 1 and d == KD - 1)
                    mm.then_inc(S("m1_h"), 1)

            def output(c_, c):
                n = rows(c)
                if c == 0:
                    c_.made(pe, S("m1_w2_lo"))
                if c >= 2:
                    c_.made(pe, S("m1_y_weighted"), SC, c - 1)
                else:
                    c_.before(pe, S("m1_y_weighted"), 1, SC, c + SC - 1)
                for f in range(FC1):
                    if c == 0:
                        c_.made(pe, S("m1_hl"), FC1, f + 1)
                    for j, (part, w) in enumerate([(hh, w2[0]), (hh, w2[1]), (hl, w2[0])]):
                        mm = pe.matmul(bank[B_Y + c % 2][0:n, 0:D], part[:, f, c * P:c * P + n], w[:, f],
                                       start=f == 0 and j == 0, stop=f == FC1 - 1 and j == 2)
                mm.then_inc(S("m1_y"), 1)

            def turn(x_, r):
                pe.wait_ge(S(f"m1_x{x_.par}_{r}"), (x_.lap() + 1) * 32)
                if r >= 2:
                    x_.made(pe, S("m1_xl"), ROUNDS, r - 1)
                else:
                    x_.before(pe, S("m1_xl"), 1, ROUNDS)
                for d in range(KD):
                    for c in (2 * r, 2 * r + 1):
                        n = rows(c)
                        at_ = d * 2 * P + (c % 2) * P
                        mm = pe.transpose(bank[B_X + r % 2][:, at_:at_ + n], x[0:n, x_.par, c, d * P:(d + 1) * P],
                                          k.ident[0:n, 0:n])
                mm.then_inc(S("m1_x_turned"), 1)

            def body(at):
                x_, c_ = at(0), at(1)
                if c_:
                    hidden(c_)
                for c in range(SC):
                    if c_:
                        output(c_, c)
                    if x_ and c < ROUNDS:
                        turn(x_, c)
            steps(pe, body, E1, DEPTH, FIRST)

        @block.scalar
        def _(act):
            act.preload_act_table(ACT.Silu)

            def upper(e, n):
                e.made(act, S(f"m1_raw{n}"), 16)
                e.before(act, S("m1_h" if n == 1 else "m1_y"), 1, FC1 if n == 1 else SC)
                act.copy(hi[n - 1][:], raw[n - 1][:]).then_inc(S(f"m1_w{n}_hi"), 1)

            def body(at):
                x_, c_ = at(0), at(1)
                if c_:
                    for f in range(FC1):
                        if f >= 2:
                            c_.made(act, S("m1_hl"), FC1, f - 1)
                        else:
                            c_.before(act, S("m1_hl"), 1, FC1, f + FC1 - 1)
                        c_.made(act, S("m1_h"), FC1, f + 1)
                        act.activation(hf[:, f % 2].rearrange("p (s n) -> p s n", s=2),
                                       k.psum[:, B_H + 2 * (f % 2):B_H + 2 * (f % 2) + 2, 0:HALF], ACT.Silu
                                       ).then_inc(S("m1_hf"), 1)
                        if f == 0:
                            c_.before(act, S("m1_y"), 1, SC)
                        c_.made(act, S("m1_hf"), FC1, f + 1)
                        act.copy(hh[:, f], hf[:, f % 2]).then_inc(S("m1_hh"), 1)
                        if f == 1:
                            upper(c_, 2)
                if x_:
                    upper(x_, 1)
                    for r in range(ROUNDS):
                        x_.made(act, S("m1_x_turned"), ROUNDS, r + 1)
                        x_.before(act, S("m1_h"), 1, FC1)
                        to, held = turned(r, xh, r % 2)
                        act.copy(to, held).then_inc(S("m1_xh"), 1)
            steps(act, body, E1, DEPTH, FIRST)

        @block.vector
        def _(dve):
            def lower(e, n):
                e.made(dve, S(f"m1_w{n}_hi"))
                dve.tensor_tensor(lo[n - 1][:], raw[n - 1][:], hi[n - 1][:].bitcast(F32), ALU.subtract
                                  ).then_inc(S(f"m1_w{n}_lo"), 1)

            def weigh(c_, c):
                n = rows(c)
                c_.made(dve, S("m1_y"), SC, c + 1)
                if c == 0:
                    dve.wait_ge(S(f"m1_slots{c_.par}"), c_.lap() * 16 + 16)
                    c_.before(dve, S("m1_added"), 1, ALL)
                dve.tensor_scalar(yw[0:n, c], bank[B_Y + c % 2][0:n, 0:D], slots[0:n, c_.par, c, 1:2].bitcast(F32), None,
                                  ALU.mult).then_inc(S("m1_y_weighted"), 1)

            def body(at):
                x_, c_ = at(0), at(1)
                if c_:
                    for f in range(FC1):
                        c_.made(dve, S("m1_hh"), FC1, f + 1)
                        dve.tensor_tensor(hl[:, f], hf[:, f % 2], hh[:, f].bitcast(F32), ALU.subtract
                                          ).then_inc(S("m1_hl"), 1)
                        if f == 1:
                            lower(c_, 2)
                for c in range(SC):
                    if c == 0 and x_:
                        lower(x_, 1)
                    if c_:
                        weigh(c_, c)
                    if x_ and c < ROUNDS:
                        x_.made(dve, S("m1_xh"), ROUNDS, c + 1)
                        (to, held), (part, _) = turned(c, xl, c % 2), turned(c, xh, c % 2)
                        dve.tensor_tensor(to, held, part.bitcast(F32), ALU.subtract).then_inc(S("m1_xl"), 1)
            steps(dve, body, E1, DEPTH, FIRST)


PHASES = [setup, token_attention, head_attention, first_mixture, last_attention, second_mixture]


def build(nc, io, out, phases=None):
    with ExitStack() as ctx:
        k = Kernel(nc, ctx, io, out)
        allocate(k)
        for phase in phases or PHASES:
            phase(k)
            if phase is first_mixture:
                k.S.clear()
                k.first_ctx.close()
                k.raw = [k.sb(f"raw{n}", [P, FC1 * D], F32) for n in (1, 2)]


def host_layout(v):
    import numpy as np
    a = {n: np.asarray(x) for n, x in v.items()}

    def rows(w):
        return w.reshape(KD, P, -1).transpose(1, 0, 2)

    heads = [a[f"L0_attn_W{n}"].reshape(D, D).T for n in "qkv"]
    out = {
        "x": a["x"],
        "wqkv": np.stack([rows(w) for w in heads], 1),
        "bqk": np.stack([a[f"L0_attn_b{n}"].reshape(2, P).T for n in "qk"], 1),
        "bv": a["L0_attn_bv"].reshape(D),
        "gate": rows(a["L0_ffn_gate_w"].T),
        "bias": a["L0_ffn_bias"],
        "router": rows(a["L1_ffn_router_w"].T),
        "moe0": np.concatenate([a["L0_ffn_W1"].reshape(E0, KD, P, I0).transpose(0, 2, 1, 3).reshape(E0, P, -1),
                                a["L0_ffn_W3"].reshape(E0, KD, P, I0).transpose(0, 2, 1, 3).reshape(E0, P, -1),
                                a["L0_ffn_W2"]], 2),
        "shared": np.concatenate([rows(a["L0_ffn_sw1"].T).reshape(P, -1), rows(a["L0_ffn_sw3"].T).reshape(P, -1),
                                  a["L0_ffn_sw2"].T], 1),
        "wqkv1": np.stack([rows(a[f"L1_attn_{n}w"]) for n in "QKV"], 1),
        "w1": a["L1_ffn_w1"].reshape(E1, KD, P, I1).transpose(0, 2, 1, 3).reshape(E1, P, -1),
        "w2": a["L1_ffn_w2"].reshape(E1, FC1, P, D).transpose(0, 2, 1, 3).reshape(E1, P, -1),
    }
    return {n: np.ascontiguousarray(x) for n, x in out.items()}


def kernel(**inputs):
    import concourse.bacc as bacc
    from concourse.bass_utils import run_bass_kernel_spmd

    nc = bacc.Bacc("TRN2", target_bir_lowering=False, num_devices=1)
    arrays = host_layout(inputs)
    io = {n: nc.dram_tensor(f"in_{n}", x.shape, mybir.dt.from_np(x.dtype), kind="ExternalInput").ap()
          for n, x in arrays.items()}
    out = nc.dram_tensor("out", (TOKENS + PAD, D), F32, kind="ExternalOutput").ap()
    build(nc, io, out)
    r = run_bass_kernel_spmd(nc, [{f"in_{n}": x for n, x in arrays.items()}], core_ids=[0])
    return r.results[0]["out"][:TOKENS].reshape(TILES, P, D)
```
